# Optimizing a Trainium2 kernel written in Bass

```python
import numpy as np
import jax
import jax.numpy as jnp

def _softmax(x, axis=-1):
    return jax.nn.softmax(x, axis=axis)

def _gelu(x):
    return jax.nn.gelu(x, approximate=True)

def _silu(x):
    return jax.nn.silu(x)

def _sigmoid(x):
    return jax.nn.sigmoid(x)

def _layernorm(x, axis=-1, eps=1e-05):
    m = jnp.mean(x, axis=axis, keepdims=True)
    v = jnp.var(x, axis=axis, keepdims=True)
    return (x - m) / jnp.sqrt(v + eps)

def _scatter_add(tgt, idx, src, axis=0):
    return tgt.at[idx].add(src)

def _segment_sum(src, seg, n):
    return jax.ops.segment_sum(src, seg, n)
kernel_name = 'mk_adaln_d1_jaxref_r8_ba7110'

def setup_inputs(seed: int=0):
    np.random.seed(seed)
    _w = jnp.asarray

    def _L0_attn_setup():
        import jax, jax.numpy as jnp
        import numpy as np
        B, S, E = (2, 256, 128)
        H, D = (16, 64)

        def _attention(q, k, v):
            dtype = q.dtype
            logits = jnp.einsum('bqhd,bkhd->bhqk', q.astype(jnp.float32), k.astype(jnp.float32))
            logits = logits / jnp.sqrt(jnp.float32(q.shape[-1]))
            mask = jnp.tril(jnp.ones((q.shape[1], q.shape[1]), dtype=jnp.bool_))
            neg = jnp.asarray(-0.7 * jnp.finfo(logits.dtype).max, dtype=logits.dtype)
            logits = jnp.where(mask, logits, neg)
            probs = jax.nn.softmax(logits, axis=-1).astype(dtype)
            return jnp.einsum('bhqk,bkhd->bqhd', probs, v)
        key = jax.random.key(seed)
        k1, k2, k3 = jax.random.split(key, 3)
        x = jax.random.normal(k1, (B, S, E), dtype=jnp.float32)
        w_qkv = jax.random.normal(k2, (E, H, 3 * D), dtype=jnp.float32) * 0.01
        w_out = jax.random.normal(k3, (H, D, E), dtype=jnp.float32) * 0.01
        return {'x': x, 'w_qkv': w_qkv, 'w_out': w_out}
    _L0_attn_in = _L0_attn_setup()

    def _L0_ffn_setup():
        import jax, jax.numpy as jnp
        import numpy as np
        D_MODEL, D_FF, N_EXP = (128, 512, 8)
        key = jax.random.key(seed)
        ks = jax.random.split(key, 8)
        s = lambda fan_in: 1.0 / np.sqrt(fan_in)
        x = jax.random.normal(ks[0], (4, 256, D_MODEL), dtype=jnp.float32)
        Wr = jax.random.uniform(ks[1], (N_EXP, D_MODEL), jnp.float32, -s(D_MODEL), s(D_MODEL))
        br = jax.random.uniform(ks[2], (N_EXP,), jnp.float32, -s(D_MODEL), s(D_MODEL))
        W1 = jax.random.uniform(ks[3], (N_EXP, D_FF, D_MODEL), jnp.float32, -s(D_MODEL), s(D_MODEL))
        b1 = jax.random.uniform(ks[4], (N_EXP, D_FF), jnp.float32, -s(D_MODEL), s(D_MODEL))
        W2 = jax.random.uniform(ks[5], (N_EXP, D_MODEL, D_FF), jnp.float32, -s(D_FF), s(D_FF))
        b2 = jax.random.uniform(ks[6], (N_EXP, D_MODEL), jnp.float32, -s(D_FF), s(D_FF))
        return {'x': x, 'Wr': Wr, 'br': br, 'W1': W1, 'b1': b1, 'W2': W2, 'b2': b2}
    _L0_ffn_in = _L0_ffn_setup()
    _L0_c = _w((lambda *s: np.random.randn(*s).astype(np.float32) * 0.05)(1, 128))
    _L0_wmod = _w((lambda *s: np.random.randn(*s).astype(np.float32) * 0.05)(128, 6 * 128) * 128 ** (-0.5))
    _d = {'L0_attn_x': _L0_attn_in['x'], 'L0_attn_w_qkv': _L0_attn_in['w_qkv'], 'L0_attn_w_out': _L0_attn_in['w_out'], 'L0_ffn_Wr': _L0_ffn_in['Wr'], 'L0_ffn_br': _L0_ffn_in['br'], 'L0_ffn_W1': _L0_ffn_in['W1'], 'L0_ffn_b1': _L0_ffn_in['b1'], 'L0_ffn_W2': _L0_ffn_in['W2'], 'L0_ffn_b2': _L0_ffn_in['b2'], 'L0_c': _L0_c, 'L0_wmod': _L0_wmod}
    _x0 = _d['L0_attn_x']
    _d['L0_attn_x'] = jax.random.normal(jax.random.fold_in(jax.random.key(seed), 1), (1, 2048, 128), dtype=_x0.dtype)
    del _x0
    return _d

def reference(L0_attn_x, L0_attn_w_qkv, L0_attn_w_out, L0_ffn_Wr, L0_ffn_br, L0_ffn_W1, L0_ffn_b1, L0_ffn_W2, L0_ffn_b2, L0_c, L0_wmod):

    def _L0_attn_ref(x, w_qkv, w_out):
        import jax, jax.numpy as jnp
        import numpy as np
        B, S, E = (2, 256, 128)
        H, D = (16, 64)

        def _attention(q, k, v):
            dtype = q.dtype
            logits = jnp.einsum('bqhd,bkhd->bhqk', q.astype(jnp.float32), k.astype(jnp.float32))
            logits = logits / jnp.sqrt(jnp.float32(q.shape[-1]))
            mask = jnp.tril(jnp.ones((q.shape[1], q.shape[1]), dtype=jnp.bool_))
            neg = jnp.asarray(-0.7 * jnp.finfo(logits.dtype).max, dtype=logits.dtype)
            logits = jnp.where(mask, logits, neg)
            probs = jax.nn.softmax(logits, axis=-1).astype(dtype)
            return jnp.einsum('bhqk,bkhd->bqhd', probs, v)
        qkv = jnp.einsum('bse,ehd->bshd', x, w_qkv)
        q, k, v = jnp.split(qkv, 3, axis=-1)
        out = _attention(q, k, v)
        return jnp.einsum('bshd,hde->bse', out, w_out)

    def _L0_ffn_ref(x, Wr, br, W1, b1, W2, b2):
        import jax, jax.numpy as jnp
        import numpy as np
        D_MODEL, D_FF, N_EXP = (128, 512, 8)
        B, S, D = x.shape
        xf = x.reshape(-1, D)
        logits = xf @ Wr.T + br
        expert_idx = jnp.argmax(logits, axis=-1)
        h = jax.nn.relu(jnp.einsum('td,efd->etf', xf, W1) + b1[:, None, :])
        y = jnp.einsum('etf,edf->etd', h, W2) + b2[:, None, :]
        out = y[expert_idx, jnp.arange(xf.shape[0])]
        return out.reshape(B, S, D)
    x = L0_attn_x
    mod = (_silu(L0_c) @ L0_wmod).reshape(L0_c.shape[0], 6, 1, -1)
    sa, ca, ga, sb, cb, gb = (mod[:, 0], mod[:, 1], mod[:, 2], mod[:, 3], mod[:, 4], mod[:, 5])
    ga = (2 * (ga >= 0) - 1) * jnp.maximum(jnp.abs(ga), 0.25)
    gb = (2 * (gb >= 0) - 1) * jnp.maximum(jnp.abs(gb), 0.25)
    h = _layernorm(x, axis=-1) * (1 + ca) + sa
    x = x + ga * _L0_attn_ref(h, L0_attn_w_qkv, L0_attn_w_out)
    h = _layernorm(x, axis=-1) * (1 + cb) + sb
    x = x + gb * _L0_ffn_ref(h, L0_ffn_Wr, L0_ffn_br, L0_ffn_W1, L0_ffn_b1, L0_ffn_W2, L0_ffn_b2)
    return x

_drawn_inputs = setup_inputs


def setup_inputs(seed=0):
    import zlib

    import numpy as np

    out = dict(_drawn_inputs(seed))
    spreads = {}
    factors = {'L0_attn_w_qkv': 8.0,
     'L0_attn_w_out': 8.0,
     'L0_ffn_br': 3.139,
     'L0_ffn_b1': 8.0,
     'L0_ffn_b2': 8.0}
    for name, (base, spread) in spreads.items():
        noise = np.random.default_rng([zlib.crc32(name.encode()), seed]).standard_normal(out[name].shape)
        drawn = base * np.exp(spread * noise) if base else spread * noise
        out[name] = jnp.asarray(drawn.astype(out[name].dtype))
    for name, factor in factors.items():
        out[name] = (out[name] * factor).astype(out[name].dtype)
    return out
```

```python
from collections import namedtuple
from contextlib import ExitStack

import concourse.bass as bass
from concourse import mybir

ALU = mybir.AluOpType
ACT = mybir.ActivationFunctionType
AX = mybir.AxisListType
F32 = mybir.dt.float32
F32R = mybir.dt.float32r
BF16 = mybir.dt.bfloat16

P = 128
BANK = 512
RING = 5
QG = 256
LEAD = 3
EXP_LAG = 2
LN_EPS = 1e-5
MASKED = -2.38e38
PRIMED = 1
MOD_MIN = 0.25

Step = namedtuple("Step", "kind g h r j c bank use n")


def plan_pair(S):
    groups = S // QG
    steps, ring, waiting, counts = [], [], [], {}

    def emit(kind, g=0, h=0, r=0, j=0, c=0, takes_bank=False):
        bank = use = 0
        if takes_bank:
            bank, use = len(ring) % RING, len(ring) // RING
            while waiting and len(ring) >= RING and any(b <= len(ring) - RING for b in waiting[0][2]):
                flush(1)
            ring.append((kind, g, r, c))
        n = counts.get(kind, 0)
        counts[kind] = n + 1
        steps.append(Step(kind, g, h, r, j, c, bank, use, n))

    def flush(n):
        for _ in range(n):
            g, r, held, _ = waiting.pop(0)
            emit("exp", g=g, h=r % 2, r=r, c=held[0])
            if r == 3:
                emit("sum", g=g)

    def late():
        while waiting and len(steps) - waiting[0][3] >= EXP_LAG:
            flush(1)

    for c in range(S // BANK):
        for which in range(2):
            for h in range(2):
                emit("proj", h=h, j=which, c=c, takes_bank=True)
    for c in range(S // BANK):
        emit("vproj", c=c, takes_bank=True)

    def scores(g):
        return [(g, r, c) for r in range(4) for c in range(chunks(g))]

    def score(g, r, c):
        first = len(ring) - c
        emit("score", g=g, h=r % 2, r=r, c=c, takes_bank=True)
        if c == chunks(g) - 1:
            waiting.append((g, r, list(range(first, first + c + 1)), len(steps)))
        else:
            late()

    def turns(g):
        out = [("turn", g, 0), ("turn", g, 1), ("bcast", g, 0), ("pv", g, 0)]
        for j in range(2, 2 * g + 2):
            out += [("turn", g, j), ("pv", g, j - 1)]
        out += [("pv", g, 2 * g + 1), ("norm", g, 0)]
        if g and g % 2 == 0:
            out.insert(min(6, len(out) - 1), ("out", g, g // 2 - 1))
        return out

    for s in scores(0):
        score(*s)
    for g in range(groups):
        ahead = scores(g + 1) if g + 1 < groups else []
        for s in ahead[:LEAD]:
            score(*s)
        while waiting and waiting[0][0] == g:
            flush(1)
        ahead, turn = ahead[LEAD:], turns(g)
        done = 0
        for i, (kind, _, j) in enumerate(turn):
            while done * len(turn) < i * len(ahead):
                score(*ahead[done])
                done += 1
            late()
            while kind in ("bcast", "out") and done < len(ahead) and ahead[done][2]:
                score(*ahead[done])
                done += 1
            if kind == "out":
                emit(kind, c=j, takes_bank=True)
            else:
                emit(kind, g=g, j=j, takes_bank=kind == "bcast")
        for s in ahead[done:]:
            score(*s)
    emit("out", c=S // BANK - 1, takes_bank=True)
    uses = [sum(1 for n in range(len(ring)) if n % RING == b) for b in range(RING)]
    return steps, uses, counts


def chunks(g):
    return (2 * g + 2 + 3) // 4


def adaln_block(nc, x, w_qkv, w_out, Wr, br, W1, b1, W2, b2, c_in, wmod, out):
    _, S, E = x.shape
    _, H, D3 = w_qkv.shape
    D = D3 // 3
    NE, FF, _ = W1.shape
    T = S // P
    NC = S // BANK
    TPC = BANK // P
    FT = FF // P
    PAIRS = H // 2
    GROUPS = S // QG
    Q_SCALE = float(D) ** -0.5
    assert E == P and D == 64 and Q_SCALE == 0.125 and FF == BANK

    steps, uses, counts = plan_pair(S)
    ring_tail = [PAIRS * u for u in uses]

    with ExitStack() as ctx:
        def sb(name, shape, dt=F32):
            return ctx.enter_context(nc.sbuf_tensor(name, shape, dt))

        def sem(name):
            return ctx.enter_context(nc.semaphore(name))

        x_sb = sb("x_sb", [P, T, E])
        hT = sb("hT", [P, S])
        q_split = [sb(f"q_split{h}", [P, S], F32R) for h in range(2)]
        k_hi = [sb(f"k_hi{h}", [P, S], F32R) for h in range(2)]
        k_lo = [sb(f"k_lo{h}", [P, S], F32R) for h in range(2)]
        v_sb = sb("v_sb", [P, T, P])
        w_qk = sb("w_qk", [P, 2, 2, 2, D])
        w_v = sb("w_v", [P, 2 * D])
        wo_pair = sb("wo_pair", [P, E])
        probs = sb("probs", [P, 2, 4, S])
        pT = sb("pT", [P, 4, BANK])
        rinv_b = sb("rinv_b", [P, 2, QG])
        oT = sb("oT", [P, S])
        accT = sb("accT", [P, S])
        row_max = sb("row_max", [P, GROUPS, 4, 4])
        neg_max = sb("neg_max", [P, GROUPS, 4])
        part_sum = sb("part_sum", [P, GROUPS, 4, 4])
        row_sum = sb("row_sum", [P, GROUPS, 4])
        rinv = sb("rinv", [P, GROUPS, 4])
        rinv_hi = sb("rinv_hi", [P, 2, 4, D], F32R)
        rinv_lo = sb("rinv_lo", [P, 2, 4, D], F32R)
        ident = sb("ident", [P, P])
        ident_r = sb("ident_r", [P, P], F32R)
        ident_b = sb("ident_b", [P, P], BF16)
        causal = sb("causal", [P, P])
        causal_b = sb("causal_b", [P, P], BF16)
        w1_rows = sb("w1_rows", [P, NE * FT, E])
        w2_rows = probs[:, 1, 0:2, :].rearrange("p r s -> p (r s)").rearrange(
            "p (e f) -> p e f", e=NE)
        b1_rows = sb("b1_rows", [NE * FT, P])
        b1T = sb("b1T", [P, NE * FT])
        b2_sb = sb("b2_sb", [NE, E])
        wr_rows = sb("wr_rows", [NE, E])
        wrT = sb("wrT", [P, NE])
        br_b = sb("br_b", [P, NE])
        c_col = sb("c_col", [P, 1])
        c_exp = sb("c_exp", [P, 1])
        c_den = sb("c_den", [P, 1])
        c_rec = sb("c_rec", [P, 1])
        c_silu = sb("c_silu", [P, 1])
        wmod_sb = probs[:, 1, 3, 0:6 * E]
        mod = sb("mod", [P, 8])
        ga_sign = sb("ga_sign", [P, 1])
        ga_size = sb("ga_size", [P, 1])
        gate_a = sb("gate_a", [P, 1])
        gb_raw = sb("gb_raw", [P, E])
        gb_sign = sb("gb_sign", [P, E])
        gb_size = sb("gb_size", [P, E])
        gate_b = sb("gate_b", [P, E])
        stats = sb("stats", [P, T, 6])
        mean_var = sb("mean_var", [P, T, 2])
        var_eps = sb("var_eps", [P, T])
        std = sb("std", [P, T])
        rough = sb("rough", [P, T])
        newton = sb("newton", [P, T])
        rstd = sb("rstd", [P, T])
        logits = sb("logits", [P, T, NE])
        top = sb("top", [P, T])
        is_top = sb("is_top", [P, T, NE])
        expert_no = sb("expert_no", [P, NE])
        top_no = sb("top_no", [P, T, NE])
        first_no = sb("first_no", [P, T])
        onehot = sb("onehot", [P, T, NE])
        onehotT = pT[0:NE, :, :].rearrange("p n s -> p (n s)")

        ps_ring = ctx.enter_context(nc.psum_tensor("ps_ring", [P, RING, BANK], F32))
        ps_turn = ctx.enter_context(nc.psum_tensor("ps_turn", [P, 2, BANK], F32))
        ps_o = ctx.enter_context(nc.psum_tensor("ps_o", [P, BANK], F32))

        x_in = [sem(f"x_in{c}") for c in range(NC)]
        mod_in = sem("mod_in")
        late_in = sem("late_in")
        w2_in = sem("w2_in")
        small_turned = sem("small_turned")
        small_ready = sem("small_ready")
        ident_made = sem("ident_made")
        ident_cast = sem("ident_cast")
        dve_chain = sem("dve_chain")
        c_exp_done = sem("c_exp_done")
        silu_done = sem("silu_done")
        mod_full = sem("mod_full")
        mod_done = sem("mod_done")
        var_ready = sem("var_ready")
        sqrt_done = sem("sqrt_done")
        norm_ready = sem("norm_ready")
        turn_full = sem("turn_full")
        h_ready = sem("h_ready")
        acc_zeroed = sem("acc_zeroed")
        w_in = sem("w_in")
        wo_in = sem("wo_in")
        bank_full = [sem(f"bank_full{b}") for b in range(RING)]
        bank_free = [sem(f"bank_free{b}") for b in range(RING)]
        hi_ready = sem("hi_ready")
        max_part = sem("max_part")
        negmax_ready = sem("negmax_ready")
        sums_step = sem("sums_step")
        rinv_ready = sem("rinv_ready")
        pT_full = sem("pT_full")
        pT_by_act = sem("pT_by_act")
        pT_by_dve = sem("pT_by_dve")
        pv_done = sem("pv_done")
        o_ready = sem("o_ready")
        gated = sem("gated")
        back_full = sem("back_full")
        back_used = sem("back_used")
        w_turned = sem("w_turned")
        w_by_act = sem("w_by_act")
        w_by_dve = sem("w_by_dve")
        logits_full = sem("logits_full")
        onehot_ready = sem("onehot_ready")
        onehot_turned = sem("onehot_turned")
        onehotT_ready = sem("onehotT_ready")
        b2_full = sem("b2_full")
        b2_taken = sem("b2_taken")
        hid_full = sem("hid_full")
        hid_by_act = sem("hid_by_act")
        hid_by_dve = sem("hid_by_dve")
        y_full = sem("y_full")
        y_used = sem("y_used")
        out_ready = sem("out_ready")
        out_stored = sem("out_stored")

        x_tiles = x.rearrange("a (t p) e -> p (a t) e", p=P)
        out_tiles = out.rearrange("a (t p) e -> p (a t) e", p=P)
        w_qkv_heads = w_qkv.rearrange("e h d -> h e d")
        w_qkv_pairs = w_qkv.rearrange("e (n h) d -> n e h d", h=2)
        w_out_pairs = w_out.rearrange("(n h) d e -> n (h d) e", h=2)
        hid = [oT, accT]
        w1T = probs[:, 0, 0:2, :].rearrange("p r s -> p (r s)")
        w2T = probs[:, 0, 2:4, :].rearrange("p r s -> p (r s)").rearrange(
            "p (e f d) -> p e f d", e=NE, f=FT)
        moe = v_sb

        def width(s):
            keys = (2 * s.g + s.r // 2 + 1) * P
            return min(BANK, keys - s.c * BANK)

        block = ctx.enter_context(nc.Block())

        @block.sync
        def _(sp):
            def load_pair(pair):
                for twice in range(2):
                    for h in range(2):
                        sp.dma_start(w_qk[:, h, :, twice, :],
                                     w_qkv_heads[2 * pair + h, :, 0:2 * D].rearrange("e (j d) -> e j d", j=2)
                                     ).then_inc(w_in, 16)
                sp.dma_start(w_v[:].rearrange("e (h d) -> e h d", h=2),
                             w_qkv_pairs[pair, :, :, 2 * D:3 * D]).then_inc(w_in, 16)

            for c in range(NC):
                sp.dma_start(x_sb[:, TPC * c:TPC * c + TPC, :],
                             x_tiles[:, TPC * c:TPC * c + TPC, :]).then_inc(x_in[c], 16)
                if c == 0:
                    sp.dma_start(c_col[:], c_in.rearrange("a e -> e a")).then_inc(mod_in, 16)
                    sp.dma_start(wmod_sb, wmod).then_inc(mod_in, 16)
            load_pair(0)
            sp.dma_start(wo_pair[:], w_out_pairs[0]).then_inc(wo_in, 16)
            sp.dma_start(w1_rows[:], W1.rearrange("e (f p) d -> p (e f) d", p=P)).then_inc(late_in, 16)
            sp.dma_start(b1_rows[:], b1.rearrange("e (f p) -> (e f) p", p=P)).then_inc(late_in, 16)
            sp.dma_start(b2_sb[:], b2).then_inc(late_in, 16)
            sp.dma_start(wr_rows[:], Wr).then_inc(late_in, 16)
            sp.dma_start(br_b[:], br.rearrange("(a n) -> a n", a=1).broadcast_to([P, NE])).then_inc(late_in, 16)
            last_vproj = [s for s in steps if s.kind == "vproj"][-1]
            last_out = [s for s in steps if s.kind == "out"][-1]
            with sp.Fori(0, PAIRS - 1) as pair:
                sp.wait_ge(bank_free[last_vproj.bank], pair * uses[last_vproj.bank] + last_vproj.use + 1 + PRIMED)
                load_pair(pair + 1)
                sp.wait_ge(bank_free[last_out.bank], pair * uses[last_out.bank] + last_out.use + 1 + PRIMED)
                sp.dma_start(wo_pair[:], w_out_pairs[pair + 1]).then_inc(wo_in, 16)
            sp.wait_ge(pT_full, PAIRS * counts["turn"] + PRIMED)
            sp.dma_start(w2_rows, W2.rearrange("e d f -> d e f")).then_inc(w2_in, 16)
            for c in range(NC):
                sp.wait_ge(out_ready, c + 1)
                sp.dma_start(out_tiles[:, TPC * c:TPC * c + TPC, :],
                             moe[:, TPC * c:TPC * c + TPC, :]).then_inc(out_stored, 16)
            sp.wait_ge(out_stored, 16 * NC)

        @block.gpsimd
        def _(pool):
            nc.gpsimd.memset(ident[:], 0.0).then_inc(ident_made, 1)
            nc.gpsimd.memset(causal[:], 0.0).then_inc(ident_made, 1)
            nc.gpsimd.iota(expert_no[:], pattern=[[1, NE]], base=-NE, channel_multiplier=0,
                           allow_small_or_imprecise_dtypes=True).then_inc(ident_made, 1)
            pool.wait_ge(ident_made, 3)
            nc.gpsimd.affine_select(out=ident[:], in_=ident[:], compare_op=ALU.not_equal, fill=1.0,
                                    base=0, pattern=[[-1, P]], channel_multiplier=1).then_inc(ident_made, 1)
            nc.gpsimd.affine_select(out=causal[:], in_=causal[:], compare_op=ALU.is_ge, fill=MASKED,
                                    base=0, pattern=[[-1, P]], channel_multiplier=1).then_inc(ident_made, 1)

        @block.tensor
        def _(pe):
            for primed in (pT_full, pv_done, y_full):
                pe.sem_inc(primed, PRIMED)
            pe.wait_ge(silu_done, 1)
            for j in range(6):
                pe.matmul(ps_o[:, j:j + 1], wmod_sb[:, E * j:E * j + E], c_silu[:], start=True, stop=True)
            pe.matmul(ps_o[:, E:2 * E], c_silu[:].to_broadcast([P, P]), wmod_sb[:, 5 * E:6 * E],
                      start=True, stop=True).then_inc(mod_full, 1)

            def turn_tokens(base):
                for c in range(NC):
                    pe.wait_ge(norm_ready, base + c + 1)
                    if c >= 2:
                        pe.wait_ge(h_ready, base + c - 1)
                    for t in range(TPC):
                        m = pe.transpose(ps_turn[:, c % 2, P * t:P * t + P],
                                         accT[:, (TPC * c + t) * P:(TPC * c + t + 1) * P], ident[:])
                    m.then_inc(turn_full, 1)

            pe.wait_ge(ident_made, 5)
            turn_tokens(0)
            pe.wait_ge(ident_cast, 3)
            pe.wait_ge(h_ready, NC)
            with pe.Fori(0, PAIRS) as pair:
                def free(s):
                    pe.wait_ge(bank_free[s.bank], pair * uses[s.bank] + s.use + PRIMED)

                last_exp = {}
                for s in steps:
                    if s.kind == "proj":
                        if s.n == 0:
                            pe.wait_ge(w_in, pair * 80 + 80)
                        free(s)
                        w = w_qk[:, s.h, s.j, :, :].rearrange("e t d -> e (t d)")
                        pe.matmul(ps_ring[:, s.bank, :], w, hT[:, s.c * BANK:(s.c + 1) * BANK],
                                  start=True, stop=True).then_inc(bank_full[s.bank], 1)
                        last_proj = s
                    elif s.kind == "vproj":
                        free(s)
                        for t in range(TPC):
                            m = pe.matmul(ps_ring[:, s.bank, P * t:P * t + P],
                                          hT[:, (TPC * s.c + t) * P:(TPC * s.c + t + 1) * P],
                                          w_v[:], start=True, stop=True)
                        m.then_inc(bank_full[s.bank], 1)
                        last_vproj = s
                    elif s.kind == "score":
                        if s.n == 0:
                            pe.wait_ge(bank_free[last_proj.bank], pair * uses[last_proj.bank] + last_proj.use + 1 + PRIMED)
                        free(s)
                        w = width(s)
                        q0 = (2 * s.g + s.r // 2) * P
                        q = q_split[s.h][:, q0:q0 + P]
                        keys = slice(s.c * BANK, s.c * BANK + w)
                        pe.matmul(ps_ring[:, s.bank, 0:w], q, k_hi[s.h][:, keys], start=True, stop=False)
                        if s.c == chunks(s.g) - 1:
                            pe.matmul(ps_ring[:, s.bank, w - P:w], ident_b[:], causal_b[:], start=False, stop=False)
                        pe.matmul(ps_ring[:, s.bank, 0:w], q, k_lo[s.h][:, keys], start=False,
                                  stop=True).then_inc(bank_full[s.bank], 1)
                        last_exp[s.g] = s
                    elif s.kind == "turn":
                        if s.j == 0:
                            e = last_exp[s.g]
                            pe.wait_ge(bank_free[e.bank], pair * uses[e.bank] + e.use + 1 + PRIMED)
                        if s.n % 2 == 0:
                            pe.wait_ge(pT_by_act, pair * (counts["turn"] // 2) + s.n // 2 + PRIMED)
                        else:
                            pe.wait_ge(pT_by_dve, pair * (counts["turn"] // 2) + s.n // 2 + PRIMED)
                        for r in range(0 if s.j <= 2 * s.g else 2, 4):
                            m = pe.transpose(ps_turn[:, s.n % 2, P * r:P * r + P],
                                             probs[:, s.g % 2, r, s.j * P:s.j * P + P], ident[:])
                        m.then_inc(pT_full, 1)
                    elif s.kind == "bcast":
                        pe.wait_ge(rinv_ready, pair * GROUPS + s.g + 1)
                        free(s)
                        for u in range(2):
                            for part in (rinv_hi, rinv_lo):
                                m = pe.matmul(ps_ring[:, s.bank, P * u:P * u + P],
                                              part[:, s.g % 2, 2 * u:2 * u + 2, :].rearrange("p h d -> p (h d)"),
                                              ident_r[:], start=part is rinv_hi, stop=part is rinv_lo)
                        m.then_inc(bank_full[s.bank], 1)
                    elif s.kind == "pv":
                        if s.j == 0:
                            pe.wait_ge(o_ready, pair * GROUPS + s.g + PRIMED)
                            if s.g == 0:
                                pe.wait_ge(bank_free[last_vproj.bank],
                                           pair * uses[last_vproj.bank] + last_vproj.use + 1 + PRIMED)
                        if s.n % 2 == 0:
                            pe.wait_ge(pT_by_act, pair * (counts["turn"] // 2) + s.n // 2 + 1 + PRIMED)
                        else:
                            pe.wait_ge(pT_by_dve, pair * (counts["turn"] // 2) + s.n // 2 + 1 + PRIMED)
                        u0 = 0 if s.j <= 2 * s.g else 1
                        turned = pT[:, s.n % 4, :].rearrange("p (u h i) -> p u h i", u=2, h=2)
                        for h in range(2):
                            m = pe.matmul(ps_o[D * h:D * h + D, P * u0:QG], v_sb[:, s.j, D * h:D * h + D],
                                          turned[:, u0:2, h, :], start=(s.j == 0), stop=(s.j == 2 * s.g + 1),
                                          skip_group_check=True)
                        m.then_inc(pv_done, 1)
                    elif s.kind == "out":
                        if s.n == 0:
                            pe.wait_ge(wo_in, pair * 16 + 16)
                        pe.wait_ge(o_ready, pair * GROUPS + 2 * s.c + 2 + PRIMED)
                        free(s)
                        pe.matmul(ps_ring[:, s.bank, :], wo_pair[:], oT[:, s.c * BANK:(s.c + 1) * BANK],
                                  start=True, stop=True).then_inc(bank_full[s.bank], 1)

            pe.wait_ge(gated, 1)
            pe.wait_ge(late_in, 16 * 5)
            pe.transpose(ps_ring[:, 4, 0:NE * FT], b1_rows[:], ident[0:NE * FT, 0:NE * FT])
            pe.transpose(ps_ring[:, 4, NE * FT:NE * FT + NE], wr_rows[:], ident[0:NE, 0:NE]).then_inc(small_turned, 1)

            for c in range(NC):
                if c >= 2:
                    pe.wait_ge(back_used, c - 1)
                for t in range(TPC):
                    m = pe.transpose(ps_turn[:, c % 2, P * t:P * t + P],
                                     oT[:, (TPC * c + t) * P:(TPC * c + t + 1) * P], ident[:])
                m.then_inc(back_full, 1)

            pe.wait_ge(back_used, NC)
            turn_tokens(NC)
            pe.wait_ge(h_ready, 2 * NC)
            pe.wait_ge(small_ready, 1)
            for t in range(T):
                m = pe.matmul(ps_o[:, t * NE:t * NE + NE], hT[:, t * P:t * P + P], wrT[:], start=True, stop=True)
            m.then_inc(logits_full, 1)

            pe.wait_ge(w2_in, 16)
            for n in range(2 * NE):
                if n >= 4:
                    pe.wait_ge(w_by_act if n % 2 == 0 else w_by_dve, n // 2 - 1)
                for f in range(FT):
                    e = n // 2
                    rows = w1_rows[:, e * FT + f, :] if n % 2 == 0 else w2_rows[:, e, f * P:(f + 1) * P]
                    m = pe.transpose(ps_ring[:, n % 4, P * f:P * f + P], rows, ident[:])
                m.then_inc(w_turned, 1)
            pe.wait_ge(onehot_ready, 1)
            for c in range(NC):
                if c >= 2:
                    pe.wait_ge(onehotT_ready, c - 1)
                for t in range(TPC):
                    m = pe.transpose(ps_turn[0:NE, c % 2, P * t:P * t + P], onehot[:, TPC * c + t, :], ident[:])
                m.then_inc(onehot_turned, 1)
            pe.wait_ge(w_by_act, NE)
            pe.wait_ge(w_by_dve, NE)
            for c in range(NC):
                pe.wait_ge(onehotT_ready, c + 1)
                for t in range(TPC):
                    i = TPC * c + t
                    m = pe.matmul(ps_ring[:, c, P * t:P * t + P], onehotT[:, P * i:P * i + P], b2_sb[:],
                                  start=True, stop=True)
                m.then_inc(b2_full, 1)
            pe.wait_ge(b2_taken, NC)

            with pe.Fori(0, NC) as c:
                def hidden(e):
                    for f in range(FT):
                        taken = max(0, (e - 1) * (FT // 2) + f // 2 + 1) if e else 0
                        pe.wait_ge(hid_by_act if f % 2 == 0 else hid_by_dve, c * (NE * FT // 2) + taken + PRIMED)
                        pe.matmul(ps_ring[:, f, :], w1T[:, (e * FT + f) * P:(e * FT + f + 1) * P],
                                  hT[:, bass.ds(c * BANK, BANK)], start=True, stop=True).then_inc(hid_full, 1)

                def output(e):
                    pe.wait_ge(hid_by_act, c * (NE * FT // 2) + (e + 1) * (FT // 2) + PRIMED)
                    pe.wait_ge(hid_by_dve, c * (NE * FT // 2) + (e + 1) * (FT // 2) + PRIMED)
                    pe.wait_ge(y_used, c * NE + max(0, e - 1) + PRIMED)
                    for t in range(TPC):
                        for f in range(FT):
                            m = pe.matmul(ps_turn[:, e % 2, P * t:P * t + P],
                                          hid[e % 2][:, f * BANK + t * P:f * BANK + (t + 1) * P],
                                          w2T[:, e, f, :], start=(f == 0), stop=(f == FT - 1))
                    m.then_inc(y_full, 1)

                hidden(0)
                for e in range(1, NE):
                    hidden(e)
                    output(e - 1)
                output(NE - 1)

        @block.scalar
        def _(act):
            for primed in (pT_by_act, hid_by_act):
                act.sem_inc(primed, PRIMED)
            act.wait_ge(mod_in, 32)
            act.activation(c_exp[:], c_col[:], ACT.Exp, scale=-1.0).then_inc(c_exp_done, 1)

            def take_h(base, scale_col, bias_col):
                act.wait_ge(var_ready, base // NC + 1)
                act.activation(std[:], var_eps[:], ACT.Sqrt).then_inc(sqrt_done, 1)
                act.wait_ge(mod_done, 1)
                for c in range(NC):
                    act.wait_ge(turn_full, base + c + 1)
                    act.activation(hT[:, c * BANK:(c + 1) * BANK], ps_turn[:, c % 2, :], ACT.Identity,
                                   bias=mod[:, bias_col:bias_col + 1],
                                   scale=mod[:, scale_col:scale_col + 1]).then_inc(h_ready, 1)

            take_h(0, 6, 0)
            with act.Fori(0, PAIRS) as pair:
                def full(s):
                    act.wait_ge(bank_full[s.bank], pair * uses[s.bank] + s.use + 1)

                rows = {(s.g, s.r, s.c): s for s in steps if s.kind == "score"}
                for s in steps:
                    if s.kind == "proj":
                        full(s)
                        dst = (q_split if s.j == 0 else k_hi)[s.h][:, s.c * BANK:(s.c + 1) * BANK]
                        act.mul(dst, ps_ring[:, s.bank, :], Q_SCALE if s.j == 0 else 1.0).then_inc(hi_ready, 1)
                    elif s.kind == "vproj":
                        full(s)
                        act.copy(v_sb[:, TPC * s.c:TPC * s.c + TPC, :].rearrange("p t d -> p (t d)"),
                                 ps_ring[:, s.bank, :]).then_inc(bank_free[s.bank], 1)
                    elif s.kind == "exp":
                        act.wait_ge(negmax_ready, pair * (4 * GROUPS) + 4 * s.g + s.r + 1)
                        if s.r == 0:
                            turned = sum(2 * g + 2 for g in range(s.g - 1))
                            act.wait_ge(pT_full, pair * counts["turn"] + turned + PRIMED)
                        for c in range(chunks(s.g)):
                            sc = rows[(s.g, s.r, c)]
                            w = width(sc)
                            act.activation(probs[:, s.g % 2, s.r, c * BANK:c * BANK + w],
                                           ps_ring[:, sc.bank, 0:w], ACT.Exp, bias=neg_max[:, s.g, s.r:s.r + 1],
                                           accum_out=part_sum[:, s.g, s.r, c:c + 1]).then_inc(bank_free[sc.bank], 1)
                    elif s.kind == "turn" and s.n % 2 == 0:
                        act.wait_ge(pT_full, pair * counts["turn"] + s.n + 1 + PRIMED)
                        act.wait_ge(pv_done, pair * counts["pv"] + max(0, s.n - 3) + PRIMED)
                        lo = 0 if s.j <= 2 * s.g else QG
                        act.copy(pT[:, s.n % 4, lo:BANK], ps_turn[:, s.n % 2, lo:BANK]).then_inc(pT_by_act, 1)
                    elif s.kind == "bcast":
                        full(s)
                        act.wait_ge(o_ready, pair * GROUPS + max(0, s.g - 1) + PRIMED)
                        act.copy(rinv_b[:, s.g % 2, :], ps_ring[:, s.bank, 0:QG]).then_inc(bank_free[s.bank], 1)

            take_h(NC, 7, 3)
            for n in range(0, 2 * NE, 2):
                act.wait_ge(w_turned, n + 1)
                act.copy(w1T[:, n // 2 * FF:(n // 2 + 1) * FF], ps_ring[:, n % 4, :]).then_inc(w_by_act, 1)
            for c in range(NC):
                act.wait_ge(onehot_turned, c + 1)
                act.copy(onehotT[:, c * BANK:(c + 1) * BANK], ps_turn[0:NE, c % 2, :]).then_inc(onehotT_ready, 1)
            for c in range(NC):
                act.wait_ge(b2_full, c + 1)
                act.copy(moe[:, TPC * c:TPC * c + TPC, :].rearrange("p t d -> p (t d)"),
                         ps_ring[:, c, :]).then_inc(b2_taken, 1)
            act.wait_ge(small_ready, 1)
            with act.Fori(0, NC) as c:
                for e in range(NE):
                    for f in range(0, FT, 2):
                        act.wait_ge(hid_full, c * (NE * FT) + e * FT + f + 1)
                        if f == 0:
                            act.wait_ge(y_full, c * NE + max(0, e - 1) + PRIMED)
                        act.activation(hid[e % 2][:, f * BANK:(f + 1) * BANK], ps_ring[:, f, :], ACT.Relu,
                                       bias=b1T[:, e * FT + f:e * FT + f + 1]).then_inc(hid_by_act, 1)

        @block.vector
        def _(dve):
            chained = [0]

            def link(ins):
                chained[0] += 1
                ins.then_inc(dve_chain, 1)
                dve.wait_ge(dve_chain, chained[0])

            for primed in [pT_by_dve, o_ready, hid_by_dve, y_used] + bank_free:
                dve.sem_inc(primed, PRIMED)
            dve.wait_ge(c_exp_done, 1)
            link(dve.tensor_scalar(c_den[:], c_exp[:], 1.0, None, ALU.add))
            link(dve.reciprocal(c_rec[:], c_den[:]))
            dve.tensor_tensor(c_silu[:], c_rec[:], c_col[:], ALU.mult).then_inc(silu_done, 1)

            def normalise(time):
                for c in range(NC):
                    if time == 0:
                        dve.wait_ge(x_in[c], 16)
                    for t in range(TPC * c, TPC * c + TPC):
                        m = dve.bn_stats(stats[:, t, :], x_sb[:, t, :])
                link(m)
                for t in range(T):
                    m = dve.bn_aggr(mean_var[:, t, :], stats[:, t, :])
                link(m)
                dve.tensor_scalar(var_eps[:], mean_var[:, :, 1], LN_EPS, None, ALU.add).then_inc(var_ready, 1)
                dve.wait_ge(var_ready, time + 1)
                dve.wait_ge(sqrt_done, time + 1)
                link(dve.reciprocal(rough[:], std[:]))
                link(dve.tensor_tensor(newton[:], rough[:], rough[:], ALU.mult))
                link(dve.tensor_tensor(newton[:], newton[:], var_eps[:], ALU.mult))
                link(dve.tensor_scalar(newton[:], newton[:], -0.5, 1.5, ALU.mult, ALU.add))
                link(dve.tensor_tensor(rstd[:], rough[:], newton[:], ALU.mult))
                for t in range(T):
                    m = dve.tensor_scalar(accT[:, t * P:(t + 1) * P], x_sb[:, t, :], mean_var[:, t, 0:1],
                                          rstd[:, t:t + 1], ALU.subtract, ALU.mult)
                    if t % TPC == TPC - 1:
                        m.then_inc(norm_ready, 1)

            normalise(0)
            dve.wait_ge(mod_full, 1)
            link(dve.tensor_copy(mod[:, 0:6], ps_o[:, 0:6]))
            dve.tensor_copy(gb_raw[:], ps_o[:, E:2 * E])
            dve.tensor_scalar(mod[:, 7:8], mod[:, 4:5], 1.0, None, ALU.add)
            link(dve.tensor_scalar(mod[:, 6:7], mod[:, 1:2], 1.0, None, ALU.add))
            gates = ((gate_a, ga_sign, ga_size, mod[:, 2:3]), (gate_b, gb_sign, gb_size, gb_raw[:]))
            for gate, sign, size, g in gates:
                m = dve.tensor_scalar(sign[:], g, 0.0, 2.0, ALU.is_ge, ALU.mult)
            link(m)
            for gate, sign, size, g in gates:
                m = dve.scalar_tensor_tensor(out=size[:], in0=sign[:], scalar=-1.0, in1=g, op0=ALU.add, op1=ALU.mult)
            link(m)
            for gate, sign, size, g in gates:
                m = dve.tensor_scalar(size[:], size[:], MOD_MIN, None, ALU.max)
            link(m)
            for gate, sign, size, g in gates:
                m = dve.scalar_tensor_tensor(out=gate[:], in0=sign[:], scalar=-1.0, in1=size[:],
                                             op0=ALU.add, op1=ALU.mult)
            m.then_inc(mod_done, 1)
            dve.wait_ge(ident_made, 5)
            dve.tensor_copy(ident_r[:], ident[:]).then_inc(ident_cast, 1)
            dve.tensor_copy(ident_b[:], ident[:]).then_inc(ident_cast, 1)
            dve.tensor_copy(causal_b[:], causal[:]).then_inc(ident_cast, 1)
            dve.wait_ge(turn_full, NC)
            dve.memset(accT[:], 0.0).then_inc(acc_zeroed, 1)
            dve.wait_ge(acc_zeroed, 1)

            parts_per_pair = sum(4 * chunks(g) + (4 if chunks(g) > 1 else 0) for g in range(GROUPS))
            with dve.Fori(0, PAIRS) as pair:
                def full(s):
                    dve.wait_ge(bank_full[s.bank], pair * uses[s.bank] + s.use + 1)

                parts = 0
                scored = {(s.g, s.r, s.c): s for s in steps if s.kind == "score"}
                for s in steps:
                    if s.kind == "proj":
                        dve.wait_ge(hi_ready, pair * counts["proj"] + s.n + 1)
                        cols = slice(s.c * BANK, (s.c + 1) * BANK)
                        if s.j == 0:
                            q = q_split[s.h][D:P, cols]
                            dve.scalar_tensor_tensor(out=q, in0=ps_ring[D:P, s.bank, :], scalar=Q_SCALE,
                                                     in1=q.bitcast(F32), op0=ALU.mult,
                                                     op1=ALU.subtract).then_inc(bank_free[s.bank], 1)
                        else:
                            dve.tensor_tensor(k_lo[s.h][:, cols], ps_ring[:, s.bank, :],
                                              k_hi[s.h][:, cols].bitcast(F32),
                                              ALU.subtract).then_inc(bank_free[s.bank], 1)
                    elif s.kind == "score":
                        full(s)
                        w, row = width(s), 4 * s.g + s.r
                        n = chunks(s.g)
                        if n == 1:
                            dve.tensor_reduce(neg_max[:, s.g, s.r:s.r + 1], ps_ring[:, s.bank, 0:w], AX.X,
                                              ALU.max, negate=True).then_inc(negmax_ready, 1)
                        else:
                            dve.tensor_reduce(row_max[:, s.g, s.r, s.c:s.c + 1], ps_ring[:, s.bank, 0:w],
                                              AX.X, ALU.max).then_inc(max_part, 1)
                            parts += 1
                            if s.c == n - 1:
                                dve.wait_ge(max_part, pair * sum(4 * chunks(g) for g in range(GROUPS) if chunks(g) > 1)
                                            + parts)
                                dve.tensor_reduce(neg_max[:, s.g, s.r:s.r + 1], row_max[:, s.g, s.r, 0:n], AX.X,
                                                  ALU.max, negate=True).then_inc(negmax_ready, 1)
                    elif s.kind == "sum":
                        last = scored[(s.g, 3, chunks(s.g) - 1)]
                        dve.wait_ge(bank_free[last.bank], pair * uses[last.bank] + last.use + 1 + PRIMED)
                        at = pair * (3 * GROUPS) + 3 * s.g
                        dve.tensor_reduce(row_sum[:, s.g, :], part_sum[:, s.g, :, 0:chunks(s.g)], AX.X,
                                          ALU.add).then_inc(sums_step, 1)
                        dve.wait_ge(sums_step, at + 1)
                        dve.reciprocal(rinv[:, s.g, :], row_sum[:, s.g, :]).then_inc(sums_step, 1)
                        dve.wait_ge(sums_step, at + 2)
                        wide = rinv[:, s.g, :].unsqueeze(2).broadcast_to([P, 4, D])
                        dve.tensor_copy(rinv_hi[:, s.g % 2], wide).then_inc(sums_step, 1)
                        dve.wait_ge(sums_step, at + 3)
                        dve.tensor_tensor(rinv_lo[:, s.g % 2], wide, rinv_hi[:, s.g % 2].bitcast(F32),
                                          ALU.subtract).then_inc(rinv_ready, 1)
                    elif s.kind == "turn" and s.n % 2 == 1:
                        dve.wait_ge(pT_full, pair * counts["turn"] + s.n + 1 + PRIMED)
                        dve.wait_ge(pv_done, pair * counts["pv"] + max(0, s.n - 3) + PRIMED)
                        lo = 0 if s.j <= 2 * s.g else QG
                        dve.tensor_copy(pT[:, s.n % 4, lo:BANK], ps_turn[:, s.n % 2, lo:BANK]).then_inc(pT_by_dve, 1)
                    elif s.kind == "bcast":
                        bcast = s
                    elif s.kind == "norm":
                        dve.wait_ge(pv_done, pair * counts["pv"] + sum(2 * g + 2 for g in range(s.g + 1)) + PRIMED)
                        dve.wait_ge(bank_free[bcast.bank], pair * uses[bcast.bank] + bcast.use + 1 + PRIMED)
                        dve.tensor_tensor(oT[:, s.g * QG:(s.g + 1) * QG], ps_o[:, 0:QG], rinv_b[:, s.g % 2, :],
                                          ALU.mult).then_inc(o_ready, 1)
                    elif s.kind == "out":
                        full(s)
                        cols = slice(s.c * BANK, (s.c + 1) * BANK)
                        dve.tensor_tensor(accT[:, cols], ps_ring[:, s.bank, :], accT[:, cols],
                                          ALU.add).then_inc(bank_free[s.bank], 1)

            for b in range(RING):
                dve.wait_ge(bank_free[b], ring_tail[b] + PRIMED)
            dve.tensor_scalar(oT[:], accT[:], gate_a[:, 0:1], None, ALU.mult).then_inc(gated, 1)
            for c in range(NC):
                dve.wait_ge(back_full, c + 1)
                xs = x_sb[:, TPC * c:TPC * c + TPC, :].rearrange("p t d -> p (t d)")
                dve.tensor_tensor(xs, ps_turn[:, c % 2, :], xs, ALU.add).then_inc(back_used, 1)
            dve.wait_ge(small_turned, 1)
            dve.tensor_copy(b1T[:], ps_ring[:, 4, 0:NE * FT])
            dve.tensor_copy(wrT[:], ps_ring[:, 4, NE * FT:NE * FT + NE]).then_inc(small_ready, 1)
            dve.wait_ge(back_used, NC)
            normalise(1)
            dve.wait_ge(logits_full, 1)
            dve.wait_ge(late_in, 16 * 5)
            link(dve.tensor_tensor(logits[:], ps_o[:, 0:T * NE].rearrange("p (t n) -> p t n", t=T),
                                   br_b[:].unsqueeze(1).broadcast_to([P, T, NE]), ALU.add))
            link(dve.tensor_reduce(top[:], logits[:], AX.X, ALU.max))
            link(dve.tensor_tensor(is_top[:], logits[:], top[:].unsqueeze(2).broadcast_to([P, T, NE]), ALU.is_equal))
            link(dve.tensor_tensor(top_no[:], is_top[:], expert_no[:].unsqueeze(1).broadcast_to([P, T, NE]), ALU.mult))
            link(dve.tensor_reduce(first_no[:], top_no[:], AX.X, ALU.min))
            dve.tensor_tensor(onehot[:], expert_no[:].unsqueeze(1).broadcast_to([P, T, NE]),
                              first_no[:].unsqueeze(2).broadcast_to([P, T, NE]), ALU.is_equal).then_inc(onehot_ready, 1)

            for n in range(1, 2 * NE, 2):
                dve.wait_ge(w_turned, n + 1)
                dve.tensor_copy(w2T[:, n // 2, :, :].rearrange("p f d -> p (f d)"),
                                ps_ring[:, n % 4, :]).then_inc(w_by_dve, 1)
            dve.wait_ge(b2_taken, NC)
            dve.wait_ge(onehot_ready, 1)
            with dve.Fori(0, NC) as c:
                def hidden(e):
                    for f in range(1, FT, 2):
                        dve.wait_ge(hid_full, c * (NE * FT) + e * FT + f + 1)
                        if f == 1:
                            dve.wait_ge(y_full, c * NE + max(0, e - 1) + PRIMED)
                        dve.tensor_scalar(hid[e % 2][:, f * BANK:(f + 1) * BANK], ps_ring[:, f, :],
                                          b1T[:, e * FT + f:e * FT + f + 1], 0.0, ALU.add,
                                          ALU.max).then_inc(hid_by_dve, 1)

                def add(e):
                    dve.wait_ge(y_full, c * NE + e + 1 + PRIMED)
                    dve.wait_ge(y_used, c * NE + e + PRIMED)
                    for t in range(TPC):
                        sum_t = moe[:, bass.ds(c * TPC + t, 1), :]
                        m = dve.scalar_tensor_tensor(
                            out=sum_t, in0=ps_turn[:, e % 2, P * t:P * t + P].unsqueeze(1),
                            scalar=onehot[:, bass.ds(c * TPC + t, 1), e],
                            in1=sum_t, op0=ALU.mult, op1=ALU.add)
                    m.then_inc(y_used, 1)

                hidden(0)
                for e in range(1, NE):
                    hidden(e)
                    add(e - 1)
                add(NE - 1)

            dve.wait_ge(y_used, NC * NE + PRIMED)
            for c in range(NC):
                part = moe[:, TPC * c:TPC * c + TPC, :]
                link(dve.tensor_tensor(part, part, gate_b[:].unsqueeze(1).broadcast_to([P, TPC, E]), ALU.mult))
                dve.tensor_tensor(part, part, x_sb[:, TPC * c:TPC * c + TPC, :], ALU.add).then_inc(out_ready, 1)


_INS = ['L0_attn_x', 'L0_attn_w_qkv', 'L0_attn_w_out', 'L0_ffn_Wr', 'L0_ffn_br', 'L0_ffn_W1', 'L0_ffn_b1',
        'L0_ffn_W2', 'L0_ffn_b2', 'L0_c', 'L0_wmod']
_OUTS = [((1, 2048, 128), 'float32')]


def kernel(**inputs):
    import numpy as _np
    import concourse.bacc as _bacc
    from concourse import mybir as _mybir
    from concourse.bass_utils import run_bass_kernel_spmd as _run

    nc = _bacc.Bacc("TRN2", target_bir_lowering=False, num_devices=1)
    arrays, args = {}, []
    for name in _INS:
        a = _np.ascontiguousarray(inputs[name])
        arrays[f"in_{name}_dram"] = a
        args.append(nc.dram_tensor(f"in_{name}_dram", a.shape, _mybir.dt.from_np(a.dtype), kind="ExternalInput").ap())
    for i, (shape, dtype) in enumerate(_OUTS):
        dt = _mybir.dt.from_np(_np.dtype(dtype))
        args.append(nc.dram_tensor(f"out_{i}_dram", shape, dt, kind="ExternalOutput").ap())
    adaln_block(nc, *args)
    r = _run(nc, [arrays], core_ids=[0])
    got = tuple(r.results[0][f"out_{i}_dram"] for i in range(len(_OUTS)))
    return got[0]
```

```python
from collections import namedtuple
from contextlib import ExitStack

import concourse.bass as bass
from concourse import mybir

ALU = mybir.AluOpType
ACT = mybir.ActivationFunctionType
AX = mybir.AxisListType
F32 = mybir.dt.float32
F32R = mybir.dt.float32r
I32 = mybir.dt.int32

P = 128
BANK = 512
RING = 4
TURN_BANKS = 3
TURN_BY_ACT = (True, True, False)
QG = 256
FRONT = 0.7
EXP_LAG = 2
OUT_AT = 3
PROJ_SPAN = 0.8
PV_LAG = 2
NEXT_PROJ = (0.1, 0.25, 0.5)
NEXT_SCORES = (0.6, 0.75, 0.9, 1.1)
LN_EPS = 1e-5
MASKED = -2.38e38
LOWEST = -3.4e38
PRIMED = 1
MOD_MIN = 0.25

Step = namedtuple("Step", "kind own g h r j c bank use n")


def plan_pairs(S):
    groups = S // QG
    used, counts = [0] * RING, {}
    waiting, steps = [], []
    taken = [0]

    def emit(kind, own=0, g=0, h=0, r=0, j=0, c=0):
        bank = use = 0
        if kind in ("proj", "vproj", "score", "bcast", "out"):
            bank = taken[0] % RING
            taken[0] += 1
            use = used[bank]
            used[bank] += 1
        n = counts.get((kind, own), 0)
        counts[kind, own] = n + 1
        steps.append(Step(kind, own, g, h, r, j, c, bank, use, n))

    def finish_row():
        own, g, r, _ = waiting.pop(0)
        emit("exp", own=own, g=g, h=r % 2, r=r)
        if r == 3:
            emit("sum", own=own, g=g)

    def run(items):
        for kind, at in items:
            while kind == "turn" and waiting and waiting[0][1] == at["g"]:
                finish_row()
            emit(kind, **at)
            if kind == "score" and at["c"] == chunks(at["g"]) - 1:
                waiting.append((at.get("own", 0), at["g"], at["r"], len(steps)))
            while waiting and len(steps) - waiting[0][3] >= EXP_LAG:
                finish_row()
        while waiting:
            finish_row()

    def project(c, own=0):
        return [("proj", dict(own=own, j=j, c=c)) for j in range(2)] + [("vproj", dict(own=own, c=c))]

    def scores(g, own=0):
        return [("score", dict(own=own, g=g, h=r % 2, r=r, c=c)) for r in range(4) for c in range(chunks(g))]

    run(project(0) + scores(0))
    before, before_used = list(steps), list(used)
    steps.clear()

    timed, late = [], []
    for g in range(groups):
        tiles = 2 * g + 2
        for j in range(tiles):
            now = g + (j + 0.5) / tiles
            timed.append((now, ("turn", dict(g=g, j=j))))
            if j == 1:
                timed.append((now, ("bcast", dict(g=g))))
            late.append([("pv", dict(g=g, j=j))] + ([("norm", dict(g=g))] if j == tiles - 1 else []))
            if len(late) > PV_LAG:
                timed += [(now, item) for item in late.pop(0)]
            if g and g % 2 == 0 and j == OUT_AT:
                timed.append((now, ("out", dict(c=g // 2 - 1))))
    for i, items in enumerate(late):
        timed += [(groups + 0.05 * i, item) for item in items]
    timed.append((groups + 1, ("out", dict(c=S // BANK - 1))))
    for g in range(1, groups):
        ahead = scores(g)
        timed += [(g - 1 + FRONT * (i + 0.5) / len(ahead), item) for i, item in enumerate(ahead)]
    for c in range(1, S // BANK):
        timed += [(2 * c - 2 + PROJ_SPAN * (i + 0.5) / 3, item) for i, item in enumerate(project(c))]
    timed += [(groups - 1 + at, item) for at, item in zip(NEXT_PROJ, project(0, own=1))]
    timed += [(groups - 1 + at, item) for at, item in zip(NEXT_SCORES, scores(0, own=1))]
    taken[0] = 0
    run([item for _, item in sorted(timed, key=lambda entry: entry[0])])
    uses = [a - b for a, b in zip(used, before_used)]
    totals = {kind: sum(1 for s in before + steps if s.kind == kind and not s.own) for kind, _ in counts}
    return before, steps, before_used, uses, totals


def chunks(g):
    return (2 * g + 2 + 3) // 4


def adaln_block(nc, x, w_qkv, w_out, Wr, br, W1, b1, W2, b2, c_in, wmod, out):
    _, S, E = x.shape
    _, H, D3 = w_qkv.shape
    D = D3 // 3
    NE, FF, _ = W1.shape
    T = S // P
    NC = S // BANK
    TPC = BANK // P
    FT = FF // P
    PAIRS = H // 2
    GROUPS = S // QG
    Q_SCALE = float(D) ** -0.5
    BODY = 8
    ROUNDS = -(-(T + NE - 1) // BODY)
    SLOTS = ROUNDS * BODY
    AHEAD = 3
    EXPERT = 2 * FF + FT + E
    assert E == P and D == 64 and Q_SCALE == 0.125 and FF == BANK

    before, steps, before_used, uses, counts = plan_pairs(S)
    ring_tail = [b + PAIRS * u for b, u in zip(before_used, uses)]

    with ExitStack() as ctx:
        def sb(name, shape, dt=F32):
            return ctx.enter_context(nc.sbuf_tensor(name, shape, dt))

        def sem(name):
            return ctx.enter_context(nc.semaphore(name))

        x_sb = sb("x_sb", [P, T, E])
        hT = sb("hT", [P, S])
        q_split = [sb(f"q_split{h}", [P, S], F32R) for h in range(2)]
        k_split = [sb(f"k_split{h}", [P, 2, S], F32R) for h in range(2)]
        v_sb = sb("v_sb", [P, T, P])
        w_pair = sb("w_pair", [P, 3, 2 * D])
        wo_pair = sb("wo_pair", [P, E])
        probs = sb("probs", [P, 2, 4, S])
        pT = sb("pT", [P, TURN_BANKS, BANK])
        rinv_b = sb("rinv_b", [P, 2, QG])
        oT = sb("oT", [P, S])
        accT = sb("accT", [P, S])
        row_max = sb("row_max", [P, GROUPS, 4, 4])
        neg_max = sb("neg_max", [P, GROUPS, 4])
        row_sum = sb("row_sum", [P, GROUPS, 4])
        rinv = sb("rinv", [P, GROUPS, 4])
        rinv_hi = sb("rinv_hi", [P, 2, 4, D], F32R)
        rinv_lo = sb("rinv_lo", [P, 2, 4, D], F32R)
        ident = sb("ident", [P, P])
        ident_r = sb("ident_r", [P, P], F32R)
        causal = sb("causal", [P, BANK])
        w1_rows = sb("w1_rows", [P, NE * FT, E])
        after = probs[:].rearrange("p a r s -> p (a r s)")
        experts = after[:, 0:NE * EXPERT].rearrange("p (e c) -> p e c", e=NE)
        w2_rows = after[:, NE * EXPERT:NE * EXPERT + NE * FF].rearrange(
            "p (e f) -> p e f", e=NE)
        chosen = after[:, NE * EXPERT:(NE + 4) * EXPERT].rearrange(
            "p (s c) -> p s c", s=4)
        b1_rows = sb("b1_rows", [NE * FT, P])
        wr_rows = sb("wr_rows", [NE, E])
        wrT = sb("wrT", [P, NE])
        br_b = sb("br_b", [P, NE])
        c_col = sb("c_col", [P, 1])
        c_exp = sb("c_exp", [P, 1])
        c_den = sb("c_den", [P, 1])
        c_rec = sb("c_rec", [P, 1])
        c_silu = sb("c_silu", [P, 1])
        wmod_sb = probs[:, 1, 3, 0:6 * E]
        mod = sb("mod", [P, 8])
        ga_sign = sb("ga_sign", [P, 1])
        ga_size = sb("ga_size", [P, 1])
        gate_a = sb("gate_a", [P, 1])
        gb_raw = sb("gb_raw", [P, E])
        gb_sign = sb("gb_sign", [P, E])
        gb_size = sb("gb_size", [P, E])
        gate_b = sb("gate_b", [P, E])
        stats = sb("stats", [P, T, 6])
        mean_var = sb("mean_var", [P, T, 2])
        var_eps = sb("var_eps", [P, T])
        std = sb("std", [P, T])
        rough = sb("rough", [P, T])
        newton = sb("newton", [P, T])
        rstd = sb("rstd", [P, T])
        logits = sb("logits", [P, T, NE])
        top = sb("top", [P, T])
        is_top = sb("is_top", [P, T, NE])
        expert_no = sb("expert_no", [P, NE])
        top_no = sb("top_no", [P, T, NE])
        first_no = sb("first_no", [P, T])
        onehot = sb("onehot", [P, T, NE])
        PAD_T, PAD_E = T // 2, NE // 2
        upto_t = [sb(f"upto_t{i}", [P, PAD_T + T, NE]) for i in range(2)]
        upto_e = [sb(f"upto_e{i}", [P, PAD_E + NE]) for i in range(2)]
        steps_of_p = sb("steps_of_p", [P, T])
        above = sb("above", [P, NE, T])
        slot_parts = sb("slot_parts", [P, T, NE])
        slot_f = sb("slot_f", [P, T])
        slot = sb("slot", [P, T], I32)
        tile_nos = sb("tile_nos", [P, SLOTS + AHEAD])
        ended = sb("ended", [P, SLOTS + AHEAD, NE])
        expert_f = sb("expert_f", [P, SLOTS + AHEAD])
        tile_expert = sb("tile_expert", [P, SLOTS + AHEAD], I32)
        earlier = sb("earlier", [P, P])
        ones = sb("ones", [P, P])
        zeros = sb("zeros", [P, P])
        x_sorted = nc.dram_tensor("x_sorted", [(SLOTS + 4) * P, E], F32).ap()
        y_sorted = nc.dram_tensor("y_sorted", [SLOTS * P, E], F32).ap()

        ps = ctx.enter_context(nc.psum_tensor("ps", [P, 8, BANK], F32))
        ps_ring = ps[:, 0:RING, :]
        ps_turn = ps[:, RING:RING + TURN_BANKS, :]
        ps_o = ps[:, 7, :]
        ps_five = ps[:, 0:5, :]
        ps_two = ps[:, 5:7, :]

        x_in = [sem(f"x_in{c}") for c in range(NC)]
        mod_in = sem("mod_in")
        late_in = sem("late_in")
        w2_in = sem("w2_in")
        small_turned = sem("small_turned")
        small_ready = sem("small_ready")
        ident_made = sem("ident_made")
        ident_cast = sem("ident_cast")
        dve_chain = sem("dve_chain")
        c_exp_done = sem("c_exp_done")
        silu_done = sem("silu_done")
        mod_full = sem("mod_full")
        mod_done = sem("mod_done")
        var_ready = sem("var_ready")
        sqrt_done = sem("sqrt_done")
        norm_ready = sem("norm_ready")
        turn_full = sem("turn_full")
        h_ready = sem("h_ready")
        acc_zeroed = sem("acc_zeroed")
        w_in = sem("w_in")
        wo_in = sem("wo_in")
        bank_full = [sem(f"bank_full{b}") for b in range(RING)]
        bank_free = [sem(f"bank_free{b}") for b in range(RING)]
        hi_ready = sem("hi_ready")
        k_doubled = sem("k_doubled")
        negmax_ready = sem("negmax_ready")
        masks_begun = sem("masks_begun")
        sums_step = sem("sums_step")
        rinv_ready = sem("rinv_ready")
        pT_full = sem("pT_full")
        exp_done = sem("exp_done")
        pT_taken = [sem(f"pT_taken{b}") for b in range(TURN_BANKS)]
        pv_done = sem("pv_done")
        o_ready = sem("o_ready")
        gated = sem("gated")
        back_full = sem("back_full")
        back_used = sem("back_used")
        w_turned = sem("w_turned")
        w_by_act = sem("w_by_act")
        w_by_dve = sem("w_by_dve")
        logits_full = sem("logits_full")
        onehot_ready = sem("onehot_ready")
        sort_full = sem("sort_full")
        slots_ready = sem("slots_ready")
        chosen_known = sem("chosen_known")
        scattered = sem("scattered")
        zero_made = sem("zero_made")
        zero_stored = sem("zero_stored")
        tile_read = [sem(f"tile_read{k}") for k in range(4)]
        tile_turned = sem("tile_turned")
        tile_h_ready = sem("tile_h_ready")
        expert_copied = sem("expert_copied")
        hid_full = sem("hid_full")
        hid_ready = sem("hid_ready")
        y_full = sem("y_full")
        y_taken = sem("y_taken")
        y_stored = [sem(f"y_stored{k}") for k in range(4)]
        gathered = [sem(f"gathered{c}") for c in range(NC)]
        out_ready = sem("out_ready")
        out_stored = sem("out_stored")

        x_tiles = x.rearrange("a (t p) e -> p (a t) e", p=P)
        out_tiles = out.rearrange("a (t p) e -> p (a t) e", p=P)
        w_qkv_pairs = w_qkv.rearrange("e (n h) d -> n e h d", h=2)
        w_out_pairs = w_out.rearrange("(n h) d e -> n (h d) e", h=2)
        tile_in = v_sb[:, 0:4, :]
        tile_hT = v_sb[:, 4:6, :]
        tile_y = v_sb[:, 8:12, :]
        hidT = oT[:].rearrange("p (s f n) -> p s f n", s=4, f=FT)
        y_back = accT[:].rearrange("p (t d) -> p t d", t=T)
        x_sorted_tiles = x_sorted.rearrange("(i p) d -> i p d", p=P)
        y_sorted_tiles = y_sorted.rearrange("(i p) d -> i p d", p=P)
        def width(s):
            keys = (2 * s.g + s.r // 2 + 1) * P
            return min(BANK, keys - s.c * BANK)

        def own_half(h):
            return slice(D * h, D * h + D)

        block = ctx.enter_context(nc.Block())

        @block.sync
        def _(sp):
            def load_pair(pair):
                for j in range(3):
                    sp.dma_start(w_pair[:, j, :].rearrange("e (h d) -> e h d", h=2),
                                 w_qkv_pairs[pair, :, :, j * D:(j + 1) * D]).then_inc(w_in, 16)

            for c in range(NC):
                sp.dma_start(x_sb[:, TPC * c:TPC * c + TPC, :],
                             x_tiles[:, TPC * c:TPC * c + TPC, :]).then_inc(x_in[c], 16)
                if c == 0:
                    sp.dma_start(c_col[:], c_in.rearrange("a e -> e a")).then_inc(mod_in, 16)
                    sp.dma_start(wmod_sb, wmod).then_inc(mod_in, 16)
            load_pair(0)
            sp.dma_start(wo_pair[:], w_out_pairs[0]).then_inc(wo_in, 16)
            sp.dma_start(w1_rows[:], W1.rearrange("e (f p) d -> p (e f) d", p=P)).then_inc(late_in, 16)
            sp.dma_start(b1_rows[:], b1.rearrange("e (f p) -> (e f) p", p=P)).then_inc(late_in, 16)
            sp.dma_start(wr_rows[:], Wr).then_inc(late_in, 16)
            sp.wait_ge(zero_made, 1)
            sp.dma_start(x_sorted.rearrange("(i p) d -> p i d", p=P),
                         zeros[:].unsqueeze(1).broadcast_to([P, SLOTS + 4, E])).then_inc(zero_stored, 16)
            sp.dma_start(br_b[:], br.rearrange("(a n) -> a n", a=1).broadcast_to([P, NE])).then_inc(late_in, 16)

            def serve(pair, steps, next_pair):
                for s in steps:
                    done = pair * uses[s.bank] + s.use + 1 + PRIMED
                    if s.kind == "proj" and s.j == 1:
                        sp.wait_ge(bank_free[s.bank], done)
                        cols = slice(s.c * BANK, (s.c + 1) * BANK)
                        for h in range(2):
                            sp.dma_start(k_split[h][own_half(1 - h), :, cols].bitcast(F32),
                                         k_split[h][own_half(h), :, cols].bitcast(F32)).then_inc(k_doubled, 16)
                    elif s.kind == "vproj" and s.c == NC - 1:
                        sp.wait_ge(bank_free[s.bank], done)
                        load_pair(next_pair)
                    elif s.kind == "out" and s.c == NC - 1 and next_pair is not pair:
                        sp.wait_ge(bank_free[s.bank], done)
                        sp.dma_start(wo_pair[:], w_out_pairs[next_pair]).then_inc(wo_in, 16)

            serve(0, before, 0)
            with sp.Fori(0, PAIRS - 1) as pair:
                serve(pair, steps, pair + 1)
            serve(PAIRS - 1, steps, PAIRS - 1)
            sp.wait_ge(k_doubled, 32 * (NC * PAIRS + 1))
            sp.wait_ge(exp_done, PAIRS * (4 * GROUPS) + 4)
            sp.wait_ge(pT_full, PAIRS * counts["turn"] + PRIMED)
            sp.dma_start(w2_rows, W2.rearrange("e d f -> d e f")).then_inc(w2_in, 16)
            sp.dma_start(experts[:, :, 2 * FF + FT:EXPERT],
                         b2.rearrange("(a e) d -> a e d", a=1).broadcast_to([P, NE, E])).then_inc(w2_in, 16)
            sp.wait_ge(scattered, 16 * T)
            for k in range(4):
                sp.dma_start(tile_in[:, k, :], x_sorted_tiles[k]).then_inc(tile_read[k], 16)
            with sp.Fori(0, ROUNDS) as rnd:
                for k in range(BODY):
                    sp.wait_ge(tile_turned, rnd * BODY + k + 1)
                    sp.dma_start(tile_in[:, k % 4, :],
                                 x_sorted_tiles[rnd * BODY + k + 4]).then_inc(tile_read[k % 4], 16)
                    sp.wait_ge(y_taken, rnd * BODY + k + 1 + PRIMED)
                    sp.dma_start(y_sorted_tiles[rnd * BODY + k], tile_y[:, k % 4, :]).then_inc(y_stored[k % 4], 16)
            for c in range(NC):
                sp.wait_ge(out_ready, c + 1)
                sp.dma_start(out_tiles[:, TPC * c:TPC * c + TPC, :],
                             y_back[:, TPC * c:TPC * c + TPC, :]).then_inc(out_stored, 16)
            for k in range(4):
                sp.wait_ge(tile_read[k], 16 * (SLOTS // 4 + 1))
            sp.wait_ge(out_stored, 16 * NC)

        @block.gpsimd
        def _(pool):
            nc.gpsimd.memset(ident[:], 0.0).then_inc(ident_made, 1)
            nc.gpsimd.memset(causal[:], 0.0).then_inc(ident_made, 1)
            nc.gpsimd.iota(expert_no[:], pattern=[[1, NE]], base=-NE, channel_multiplier=0,
                           allow_small_or_imprecise_dtypes=True).then_inc(ident_made, 1)
            nc.gpsimd.iota(steps_of_p[:], pattern=[[P, T]], base=0, channel_multiplier=0,
                           allow_small_or_imprecise_dtypes=True).then_inc(ident_made, 1)
            nc.gpsimd.iota(tile_nos[:], pattern=[[1, SLOTS + AHEAD]], base=0, channel_multiplier=0,
                           allow_small_or_imprecise_dtypes=True).then_inc(ident_made, 1)
            nc.gpsimd.memset(ones[:], 1.0).then_inc(ident_made, 1)
            pool.wait_ge(ident_made, 6)
            nc.gpsimd.affine_select(out=ident[:], in_=ident[:], compare_op=ALU.not_equal, fill=1.0,
                                    base=0, pattern=[[-1, P]], channel_multiplier=1).then_inc(ident_made, 1)
            nc.gpsimd.affine_select(out=causal[:, BANK - P:], in_=causal[:, BANK - P:], compare_op=ALU.is_ge, fill=MASKED,
                                    base=0, pattern=[[-1, P]], channel_multiplier=1).then_inc(ident_made, 1)
            nc.gpsimd.affine_select(out=earlier[:], in_=ones[:], compare_op=ALU.is_ge, fill=0.0,
                                    base=-1, pattern=[[1, P]], channel_multiplier=-1).then_inc(ident_made, 1)
            nc.gpsimd.memset(zeros[:], 0.0).then_inc(zero_made, 1)

            pool.wait_ge(slots_ready, 1)
            pool.wait_ge(zero_stored, 16)
            for t in range(T):
                pool.indirect_dma_start(x_sorted, bass.IndirectOffsetOnAxis(slot[:, t:t + 1], 0),
                                        accT[:, t * P:(t + 1) * P], None).then_inc(scattered, 16)
            pool.wait_ge(scattered, 16 * T)
            for k in range(4):
                pool.wait_ge(y_stored[k], 16 * (SLOTS // 4) + PRIMED)
            for t in range(T):
                pool.indirect_dma_start(y_back[:, t, :], None, y_sorted,
                                        bass.IndirectOffsetOnAxis(slot[:, t:t + 1], 0)).then_inc(gathered[t // TPC], 16)

        @block.tensor
        def _(pe):
            for primed in (pT_full, pv_done, hid_full, y_full):
                pe.sem_inc(primed, PRIMED)
            pe.wait_ge(silu_done, 1)
            for j in range(6):
                pe.matmul(ps_o[:, j:j + 1], wmod_sb[:, E * j:E * j + E], c_silu[:], start=True, stop=True)
            pe.matmul(ps_o[:, E:2 * E], c_silu[:].to_broadcast([P, P]), wmod_sb[:, 5 * E:6 * E],
                      start=True, stop=True).then_inc(mod_full, 1)

            def turn_tokens(base):
                for c in range(NC):
                    pe.wait_ge(norm_ready, base + c + 1)
                    if c >= 2:
                        pe.wait_ge(h_ready, base + c - 1)
                    for t in range(TPC):
                        m = pe.transpose(ps_two[:, c % 2, P * t:P * t + P],
                                         accT[:, (TPC * c + t) * P:(TPC * c + t + 1) * P], ident[:])
                    m.then_inc(turn_full, 1)

            pe.wait_ge(ident_made, 9)
            turn_tokens(0)
            pe.wait_ge(ident_cast, 1)
            pe.wait_ge(h_ready, NC)
            turns_per_bank = counts["turn"] // TURN_BANKS

            def run(pair, steps):
                def free(s):
                    pe.wait_ge(bank_free[s.bank], pair * uses[s.bank] + s.use + PRIMED)

                v_projected = {(s.own, s.c): s for s in steps if s.kind == "vproj"}
                for s in steps:
                    if s.kind == "proj":
                        if s.c == 0:
                            pe.wait_ge(w_in, pair * 48 + s.own * 48 + 48)
                        free(s)
                        pe.matmul(ps_ring[:, s.bank, :], w_pair[:, s.j, :], hT[:, s.c * BANK:(s.c + 1) * BANK],
                                  start=True, stop=True).then_inc(bank_full[s.bank], 1)
                    elif s.kind == "vproj":
                        free(s)
                        for t in range(TPC):
                            m = pe.matmul(ps_ring[:, s.bank, P * t:P * t + P],
                                          hT[:, (TPC * s.c + t) * P:(TPC * s.c + t + 1) * P],
                                          w_pair[:, 2, :], start=True, stop=True)
                        m.then_inc(bank_full[s.bank], 1)
                    elif s.kind == "score":
                        if s.g % 2 == 0 and s.r == 0 and s.c == 0:
                            pe.wait_ge(k_doubled, pair * (32 * NC) + 32 * (s.own * NC + s.g // 2 + 1))
                        free(s)
                        w = width(s)
                        q0 = (2 * s.g + s.r // 2) * P
                        q = q_split[s.h][:, q0:q0 + P]
                        keys = slice(s.c * BANK, s.c * BANK + w)
                        for part in range(2):
                            m = pe.matmul(ps_ring[:, s.bank, 0:w], q, k_split[s.h][:, part, keys],
                                          start=(part == 0), stop=(part == 1))
                        m.then_inc(bank_full[s.bank], 1)
                    elif s.kind == "turn":
                        if s.j == 0:
                            pe.wait_ge(exp_done, pair * (4 * GROUPS) + 4 * s.g + 4)
                        bank = s.n % TURN_BANKS
                        pe.wait_ge(pT_taken[bank], pair * turns_per_bank + s.n // TURN_BANKS + PRIMED)
                        for r in range(0 if s.j <= 2 * s.g else 2, 4):
                            m = pe.transpose(ps_turn[:, bank, P * r:P * r + P],
                                             probs[:, s.g % 2, r, s.j * P:s.j * P + P], ident[:])
                        m.then_inc(pT_full, 1)
                    elif s.kind == "bcast":
                        pe.wait_ge(rinv_ready, pair * GROUPS + s.g + 1)
                        free(s)
                        for u in range(2):
                            for part in (rinv_hi, rinv_lo):
                                m = pe.matmul(ps_ring[:, s.bank, P * u:P * u + P],
                                              part[:, s.g % 2, 2 * u:2 * u + 2, :].rearrange("p h d -> p (h d)"),
                                              ident_r[:], start=part is rinv_hi, stop=part is rinv_lo)
                        m.then_inc(bank_full[s.bank], 1)
                    elif s.kind == "pv":
                        if s.j == 0:
                            pe.wait_ge(o_ready, pair * GROUPS + s.g + PRIMED)
                            if s.g % 2 == 0 and s.g:
                                last = v_projected[0, s.g // 2]
                                pe.wait_ge(bank_free[last.bank], pair * uses[last.bank] + last.use + 1 + PRIMED)
                        bank = s.n % TURN_BANKS
                        pe.wait_ge(pT_taken[bank], pair * turns_per_bank + s.n // TURN_BANKS + 1 + PRIMED)
                        u0 = 0 if s.j <= 2 * s.g else 1
                        turned = pT[:, bank, :].rearrange("p (u h i) -> p u h i", u=2, h=2)
                        for h in range(2):
                            m = pe.matmul(ps_o[D * h:D * h + D, P * u0:QG], v_sb[:, s.j, D * h:D * h + D],
                                          turned[:, u0:2, h, :], start=(s.j == 0), stop=(s.j == 2 * s.g + 1),
                                          skip_group_check=True)
                        m.then_inc(pv_done, 1)
                    elif s.kind == "out":
                        if s.n == 0:
                            pe.wait_ge(wo_in, pair * 16 + 16)
                        pe.wait_ge(o_ready, pair * GROUPS + 2 * s.c + 2 + PRIMED)
                        free(s)
                        pe.matmul(ps_ring[:, s.bank, :], wo_pair[:], oT[:, s.c * BANK:(s.c + 1) * BANK],
                                  start=True, stop=True).then_inc(bank_full[s.bank], 1)

            run(0, before)
            with pe.Fori(0, PAIRS) as pair:
                run(pair, steps)

            pe.wait_ge(gated, 1)
            pe.wait_ge(late_in, 16 * 4)
            pe.transpose(ps_five[:, 4, 0:NE * FT], b1_rows[:], ident[0:NE * FT, 0:NE * FT])
            pe.transpose(ps_five[:, 4, NE * FT:NE * FT + NE], wr_rows[:], ident[0:NE, 0:NE]).then_inc(small_turned, 1)

            for c in range(NC):
                if c >= 2:
                    pe.wait_ge(back_used, c - 1)
                for t in range(TPC):
                    m = pe.transpose(ps_two[:, c % 2, P * t:P * t + P],
                                     oT[:, (TPC * c + t) * P:(TPC * c + t + 1) * P], ident[:])
                m.then_inc(back_full, 1)

            pe.wait_ge(back_used, NC)
            turn_tokens(NC)
            pe.wait_ge(h_ready, 2 * NC)
            pe.wait_ge(small_ready, 1)
            for t in range(T):
                m = pe.matmul(ps_o[:, t * NE:t * NE + NE], hT[:, t * P:t * P + P], wrT[:], start=True, stop=True)
            m.then_inc(logits_full, 1)

            pe.wait_ge(onehot_ready, 1)
            flat = onehot[:].rearrange("p t n -> p (t n)")
            pe.matmul(ps_two[:, 0, 0:T * NE], earlier[:], flat, start=True, stop=True)
            pe.matmul(ps_two[:, 1, 0:T * NE], ones[:], flat, start=True, stop=True).then_inc(sort_full, 1)

            pe.wait_ge(w2_in, 32)
            for n in range(2 * NE):
                if n >= 4:
                    pe.wait_ge(w_by_act if n % 2 == 0 else w_by_dve, n // 2 - 1)
                for f in range(FT):
                    e = n // 2
                    rows = w1_rows[:, e * FT + f, :] if n % 2 == 0 else w2_rows[:, e, f * P:(f + 1) * P]
                    m = pe.transpose(ps_five[:, n % 4, P * f:P * f + P], rows, ident[:])
                m.then_inc(w_turned, 1)
            pe.wait_ge(w_by_act, NE)
            pe.wait_ge(w_by_dve, NE)
            with pe.Fori(0, ROUNDS) as rnd:
                def turn(k):
                    pe.wait_ge(tile_read[k % 4], rnd * (16 * BODY // 4) + 16 * (k // 4) + 16)
                    pe.wait_ge(tile_h_ready, rnd * BODY + max(0, k - 1) + PRIMED)
                    pe.transpose(ps_two[:, k % 2, 0:P], tile_in[:, k % 4, :], ident[:]).then_inc(tile_turned, 1)

                def hidden(k):
                    pe.wait_ge(tile_h_ready, rnd * BODY + k + 1 + PRIMED)
                    pe.wait_ge(expert_copied, rnd * BODY + k + 1)
                    pe.wait_ge(hid_ready, rnd * BODY + max(0, k - 1) + PRIMED)
                    for f in range(FT):
                        m = pe.matmul(ps_five[:, k % 2, f * P:(f + 1) * P], chosen[:, k % 4, f * P:(f + 1) * P],
                                      tile_hT[:, k % 2, :], start=True, stop=True)
                    m.then_inc(hid_full, 1)

                def output(k):
                    pe.wait_ge(hid_ready, rnd * BODY + k + 1 + PRIMED)
                    pe.wait_ge(y_taken, rnd * BODY + max(0, k - 1) + PRIMED)
                    for f in range(FT):
                        m = pe.matmul(ps_five[:, 2 + k % 2, 0:E], hidT[:, k % 4, f, :],
                                      chosen[:, k % 4, FF + f * E:FF + (f + 1) * E], start=(f == 0),
                                      stop=(f == FT - 1))
                    m.then_inc(y_full, 1)

                turn(0)
                for k in range(BODY):
                    if k + 1 < BODY:
                        turn(k + 1)
                    hidden(k)
                    if k >= 2:
                        output(k - 2)
                output(BODY - 2)
                output(BODY - 1)

        @block.scalar
        def _(act):
            for primed in (tile_h_ready, hid_ready):
                act.sem_inc(primed, PRIMED)
            act.wait_ge(mod_in, 32)
            act.activation(c_exp[:], c_col[:], ACT.Exp, scale=-1.0).then_inc(c_exp_done, 1)

            def take_h(base, scale_col, bias_col):
                act.wait_ge(var_ready, base // NC + 1)
                act.activation(std[:], var_eps[:], ACT.Sqrt).then_inc(sqrt_done, 1)
                act.wait_ge(mod_done, 1)
                for c in range(NC):
                    act.wait_ge(turn_full, base + c + 1)
                    act.activation(hT[:, c * BANK:(c + 1) * BANK], ps_two[:, c % 2, :], ACT.Identity,
                                   bias=mod[:, bias_col:bias_col + 1],
                                   scale=mod[:, scale_col:scale_col + 1]).then_inc(h_ready, 1)

            take_h(0, 6, 0)

            def run(pair, steps):
                def full(s):
                    act.wait_ge(bank_full[s.bank], pair * uses[s.bank] + s.use + 1)

                for s in steps:
                    if s.kind == "proj":
                        full(s)
                        for h in range(2):
                            dst = q_split[h] if s.j == 0 else k_split[h][:, 0, :]
                            m = act.mul(dst[own_half(h), s.c * BANK:(s.c + 1) * BANK],
                                        ps_ring[own_half(h), s.bank, :], Q_SCALE if s.j == 0 else 1.0)
                        m.then_inc(hi_ready, 1)
                    elif s.kind == "vproj":
                        full(s)
                        act.copy(v_sb[:, TPC * s.c:TPC * s.c + TPC, :].rearrange("p t d -> p (t d)"),
                                 ps_ring[:, s.bank, :]).then_inc(bank_free[s.bank], 1)
                    elif s.kind == "exp":
                        act.wait_ge(negmax_ready, pair * (4 * GROUPS) + 4 * (s.own * GROUPS + s.g) + s.r + 1)
                        keys = (2 * s.g + s.r // 2 + 1) * P
                        row = probs[:, s.g % 2, s.r, 0:keys]
                        act.activation(row, row, ACT.Exp, bias=neg_max[:, s.g, s.r:s.r + 1],
                                       accum_out=row_sum[:, s.g, s.r:s.r + 1]).then_inc(exp_done, 1)
                    elif s.kind == "turn" and TURN_BY_ACT[s.n % TURN_BANKS]:
                        bank = s.n % TURN_BANKS
                        act.wait_ge(pT_full, pair * counts["turn"] + s.n + 1 + PRIMED)
                        act.wait_ge(pv_done, pair * counts["pv"] + max(0, s.n - TURN_BANKS + 1) + PRIMED)
                        lo = 0 if s.j <= 2 * s.g else QG
                        act.copy(pT[:, bank, lo:BANK], ps_turn[:, bank, lo:BANK]).then_inc(pT_taken[bank], 1)
                    elif s.kind == "bcast":
                        full(s)
                        act.wait_ge(o_ready, pair * GROUPS + max(0, s.g - 1) + PRIMED)
                        act.copy(rinv_b[:, s.g % 2, :], ps_ring[:, s.bank, 0:QG]).then_inc(bank_free[s.bank], 1)

            run(0, before)
            with act.Fori(0, PAIRS) as pair:
                run(pair, steps)

            take_h(NC, 7, 3)
            for n in range(0, 2 * NE, 2):
                act.wait_ge(w_turned, n + 1)
                act.copy(experts[:, n // 2, 0:FF], ps_five[:, n % 4, :]).then_inc(w_by_act, 1)
            with act.Fori(0, ROUNDS) as rnd:
                def modulate(k):
                    act.wait_ge(tile_turned, rnd * BODY + k + 1)
                    act.wait_ge(hid_full, rnd * BODY + max(0, k - 1) + PRIMED)
                    act.activation(tile_hT[:, k % 2, :], ps_two[:, k % 2, 0:P], ACT.Identity,
                                   bias=mod[:, 3:4], scale=mod[:, 7:8]).then_inc(tile_h_ready, 1)

                def rectify(k):
                    act.wait_ge(hid_full, rnd * BODY + k + 1 + PRIMED)
                    act.wait_ge(y_full, rnd * BODY + max(0, k - 3) + PRIMED)
                    for f in range(FT):
                        m = act.activation(hidT[:, k % 4, f, :], ps_five[:, k % 2, f * P:(f + 1) * P], ACT.Relu,
                                           bias=chosen[:, k % 4, 2 * FF + f:2 * FF + f + 1])
                    m.then_inc(hid_ready, 1)

                modulate(0)
                for k in range(BODY):
                    if k + 1 < BODY:
                        modulate(k + 1)
                    rectify(k)

        @block.vector
        def _(dve):
            chained = [0]

            def link(ins):
                chained[0] += 1
                ins.then_inc(dve_chain, 1)
                dve.wait_ge(dve_chain, chained[0])

            for primed in [o_ready, y_taken] + bank_free + pT_taken + y_stored:
                dve.sem_inc(primed, PRIMED)
            dve.wait_ge(c_exp_done, 1)
            link(dve.tensor_scalar(c_den[:], c_exp[:], 1.0, None, ALU.add))
            link(dve.reciprocal(c_rec[:], c_den[:]))
            dve.tensor_tensor(c_silu[:], c_rec[:], c_col[:], ALU.mult).then_inc(silu_done, 1)

            def normalise(time):
                for c in range(NC):
                    if time == 0:
                        dve.wait_ge(x_in[c], 16)
                    for t in range(TPC * c, TPC * c + TPC):
                        m = dve.bn_stats(stats[:, t, :], x_sb[:, t, :])
                link(m)
                for t in range(T):
                    m = dve.bn_aggr(mean_var[:, t, :], stats[:, t, :])
                link(m)
                dve.tensor_scalar(var_eps[:], mean_var[:, :, 1], LN_EPS, None, ALU.add).then_inc(var_ready, 1)
                dve.wait_ge(var_ready, time + 1)
                dve.wait_ge(sqrt_done, time + 1)
                link(dve.reciprocal(rough[:], std[:]))
                link(dve.tensor_tensor(newton[:], rough[:], rough[:], ALU.mult))
                link(dve.tensor_tensor(newton[:], newton[:], var_eps[:], ALU.mult))
                link(dve.tensor_scalar(newton[:], newton[:], -0.5, 1.5, ALU.mult, ALU.add))
                link(dve.tensor_tensor(rstd[:], rough[:], newton[:], ALU.mult))
                for t in range(T):
                    m = dve.tensor_scalar(accT[:, t * P:(t + 1) * P], x_sb[:, t, :], mean_var[:, t, 0:1],
                                          rstd[:, t:t + 1], ALU.subtract, ALU.mult)
                    if t % TPC == TPC - 1:
                        m.then_inc(norm_ready, 1)

            normalise(0)
            dve.wait_ge(mod_full, 1)
            link(dve.tensor_copy(mod[:, 0:6], ps_o[:, 0:6]))
            dve.tensor_copy(gb_raw[:], ps_o[:, E:2 * E])
            dve.tensor_scalar(mod[:, 7:8], mod[:, 4:5], 1.0, None, ALU.add)
            link(dve.tensor_scalar(mod[:, 6:7], mod[:, 1:2], 1.0, None, ALU.add))
            gates = ((gate_a, ga_sign, ga_size, mod[:, 2:3]), (gate_b, gb_sign, gb_size, gb_raw[:]))
            for gate, sign, size, g in gates:
                m = dve.tensor_scalar(sign[:], g, 0.0, 2.0, ALU.is_ge, ALU.mult)
            link(m)
            for gate, sign, size, g in gates:
                m = dve.scalar_tensor_tensor(out=size[:], in0=sign[:], scalar=-1.0, in1=g, op0=ALU.add, op1=ALU.mult)
            link(m)
            for gate, sign, size, g in gates:
                m = dve.tensor_scalar(size[:], size[:], MOD_MIN, None, ALU.max)
            link(m)
            for gate, sign, size, g in gates:
                m = dve.scalar_tensor_tensor(out=gate[:], in0=sign[:], scalar=-1.0, in1=size[:],
                                             op0=ALU.add, op1=ALU.mult)
            m.then_inc(mod_done, 1)
            dve.wait_ge(ident_made, 9)
            dve.tensor_copy(ident_r[:], ident[:]).then_inc(ident_cast, 1)
            for padded in upto_t + upto_e:
                dve.memset(padded[:], 0.0)
            dve.wait_ge(turn_full, NC)
            dve.memset(accT[:], 0.0).then_inc(acc_zeroed, 1)
            dve.wait_ge(acc_zeroed, 1)

            def run(pair, steps):
                def full(s):
                    dve.wait_ge(bank_full[s.bank], pair * uses[s.bank] + s.use + 1)

                bcast = {s.g: s for s in steps if s.kind == "bcast"}
                for s in steps:
                    if s.kind == "proj":
                        dve.wait_ge(hi_ready, pair * counts["proj"] + s.own * counts["proj"] + s.n + 1)
                        cols = slice(s.c * BANK, (s.c + 1) * BANK)
                        for h in range(2):
                            whole = ps_ring[own_half(h), s.bank, :]
                            if s.j == 0:
                                m = dve.scalar_tensor_tensor(
                                    out=q_split[h][own_half(1 - h), cols], in0=whole, scalar=Q_SCALE,
                                    in1=q_split[h][own_half(h), cols].bitcast(F32), op0=ALU.mult, op1=ALU.subtract)
                            else:
                                m = dve.tensor_tensor(k_split[h][own_half(h), 1, cols], whole,
                                                      k_split[h][own_half(h), 0, cols].bitcast(F32), ALU.subtract)
                        m.then_inc(bank_free[s.bank], 1)
                    elif s.kind == "score":
                        full(s)
                        w = width(s)
                        n = chunks(s.g)
                        if s.r == 0 and s.c == 0 and (s.g or s.own):
                            turned = sum(2 * g + 2 for g in range(s.g - 1)) if s.g else -2 * GROUPS
                            dve.wait_ge(pT_full, pair * counts["turn"] + s.own * counts["turn"] + turned + PRIMED)
                        if s.c == n - 1:
                            dve.sem_inc(masks_begun, 1)
                        row = probs[:, s.g % 2, s.r, s.c * BANK:s.c * BANK + w]
                        highest = row_max[:, s.g, s.r, s.c:s.c + 1]
                        if s.c < n - 1:
                            m = dve.tensor_scalar(row, ps_ring[:, s.bank, 0:w], 1.0, LOWEST, ALU.mult, ALU.max,
                                                  accum_out=highest)
                        else:
                            m = dve.tensor_tensor_reduce(row, ps_ring[:, s.bank, 0:w], causal[:, BANK - w:],
                                                         1.0, LOWEST, ALU.add, ALU.max, highest)
                        m.then_inc(bank_free[s.bank], 1)
                        if s.c == n - 1:
                            dve.wait_ge(bank_free[s.bank], pair * uses[s.bank] + s.use + 1 + PRIMED)
                            dve.tensor_reduce(neg_max[:, s.g, s.r:s.r + 1], row_max[:, s.g, s.r, 0:n], AX.X,
                                              ALU.max, negate=True).then_inc(negmax_ready, 1)
                    elif s.kind == "sum":
                        dve.wait_ge(exp_done, pair * (4 * GROUPS) + 4 * (s.own * GROUPS + s.g) + 4)
                        at = pair * (2 * GROUPS) + 2 * (s.own * GROUPS + s.g)
                        dve.reciprocal(rinv[:, s.g, :], row_sum[:, s.g, :]).then_inc(sums_step, 1)
                        dve.wait_ge(sums_step, at + 1)
                        wide = rinv[:, s.g, :].unsqueeze(2).broadcast_to([P, 4, D])
                        dve.tensor_copy(rinv_hi[:, s.g % 2], wide).then_inc(sums_step, 1)
                        dve.wait_ge(sums_step, at + 2)
                        dve.tensor_tensor(rinv_lo[:, s.g % 2], wide, rinv_hi[:, s.g % 2].bitcast(F32),
                                          ALU.subtract).then_inc(rinv_ready, 1)
                    elif s.kind == "turn" and not TURN_BY_ACT[s.n % TURN_BANKS]:
                        bank = s.n % TURN_BANKS
                        dve.wait_ge(pT_full, pair * counts["turn"] + s.n + 1 + PRIMED)
                        dve.wait_ge(pv_done, pair * counts["pv"] + max(0, s.n - TURN_BANKS + 1) + PRIMED)
                        lo = 0 if s.j <= 2 * s.g else QG
                        dve.tensor_copy(pT[:, bank, lo:BANK], ps_turn[:, bank, lo:BANK]).then_inc(pT_taken[bank], 1)
                    elif s.kind == "norm":
                        dve.wait_ge(pv_done, pair * counts["pv"] + sum(2 * g + 2 for g in range(s.g + 1)) + PRIMED)
                        b = bcast[s.g]
                        dve.wait_ge(bank_free[b.bank], pair * uses[b.bank] + b.use + 1 + PRIMED)
                        dve.tensor_tensor(oT[:, s.g * QG:(s.g + 1) * QG], ps_o[:, 0:QG], rinv_b[:, s.g % 2, :],
                                          ALU.mult).then_inc(o_ready, 1)
                    elif s.kind == "out":
                        full(s)
                        cols = slice(s.c * BANK, (s.c + 1) * BANK)
                        dve.tensor_tensor(accT[:, cols], ps_ring[:, s.bank, :], accT[:, cols],
                                          ALU.add).then_inc(bank_free[s.bank], 1)

            run(0, before)
            with dve.Fori(0, PAIRS) as pair:
                run(pair, steps)

            for b in range(RING):
                dve.wait_ge(bank_free[b], ring_tail[b] + PRIMED)
            dve.tensor_scalar(oT[:], accT[:], gate_a[:, 0:1], None, ALU.mult).then_inc(gated, 1)
            for c in range(NC):
                dve.wait_ge(back_full, c + 1)
                xs = x_sb[:, TPC * c:TPC * c + TPC, :].rearrange("p t d -> p (t d)")
                dve.tensor_tensor(xs, ps_two[:, c % 2, :], xs, ALU.add).then_inc(back_used, 1)
            dve.wait_ge(small_turned, 1)
            dve.tensor_copy(experts[:, :, 2 * FF:2 * FF + FT],
                            ps_five[:, 4, 0:NE * FT].rearrange("p (e f) -> p e f", e=NE))
            dve.tensor_copy(wrT[:], ps_five[:, 4, NE * FT:NE * FT + NE]).then_inc(small_ready, 1)
            dve.wait_ge(back_used, NC)
            normalise(1)
            dve.wait_ge(logits_full, 1)
            dve.wait_ge(late_in, 16 * 4)
            link(dve.tensor_tensor(logits[:], ps_o[:, 0:T * NE].rearrange("p (t n) -> p t n", t=T),
                                   br_b[:].unsqueeze(1).broadcast_to([P, T, NE]), ALU.add))
            link(dve.tensor_reduce(top[:], logits[:], AX.X, ALU.max))
            link(dve.tensor_tensor(is_top[:], logits[:], top[:].unsqueeze(2).broadcast_to([P, T, NE]), ALU.is_equal))
            link(dve.tensor_tensor(top_no[:], is_top[:], expert_no[:].unsqueeze(1).broadcast_to([P, T, NE]), ALU.mult))
            link(dve.tensor_reduce(first_no[:], top_no[:], AX.X, ALU.min))
            dve.tensor_tensor(onehot[:], expert_no[:].unsqueeze(1).broadcast_to([P, T, NE]),
                              first_no[:].unsqueeze(2).broadcast_to([P, T, NE]), ALU.is_equal).then_inc(onehot_ready, 1)


            by_t = lambda ap: ap.unsqueeze(1).broadcast_to([P, T, NE])
            dve.wait_ge(onehot_ready, 1)
            dve.wait_ge(sort_full, 1)
            link(dve.tensor_copy(upto_t[0][:, PAD_T:, :], ps_two[:, 1, 0:T * NE].rearrange("p (t n) -> p t n", t=T)))
            at, shift = 0, 1
            while shift < T:
                link(dve.tensor_tensor(upto_t[1 - at][:, PAD_T:, :], upto_t[at][:, PAD_T:, :],
                                       upto_t[at][:, PAD_T - shift:PAD_T + T - shift, :], ALU.add))
                at, shift = 1 - at, 2 * shift
            counted = upto_t[at]
            link(dve.tensor_tensor(above[:], counted[:, PAD_T + T - 1, :].unsqueeze(2).broadcast_to([P, NE, T]),
                                   steps_of_p[:].unsqueeze(1).broadcast_to([P, NE, T]), ALU.is_gt))
            link(dve.tensor_reduce(upto_e[0][:, PAD_E:], above[:], AX.X, ALU.add))
            at, shift = 0, 1
            while shift < NE:
                link(dve.tensor_tensor(upto_e[1 - at][:, PAD_E:], upto_e[at][:, PAD_E:],
                                       upto_e[at][:, PAD_E - shift:PAD_E + NE - shift], ALU.add))
                at, shift = 1 - at, 2 * shift
            ends = upto_e[at]
            link(dve.tensor_tensor(slot_parts[:], ps_two[:, 0, 0:T * NE].rearrange("p (t n) -> p t n", t=T),
                                   counted[:, PAD_T - 1:PAD_T + T - 1, :], ALU.add))
            link(dve.scalar_tensor_tensor(out=slot_parts[:], in0=by_t(ends[:, PAD_E - 1:PAD_E + NE - 1]),
                                          scalar=float(P), in1=slot_parts[:], op0=ALU.mult, op1=ALU.add))
            link(dve.tensor_tensor(slot_parts[:], slot_parts[:], onehot[:], ALU.mult))
            link(dve.tensor_reduce(slot_f[:], slot_parts[:], AX.X, ALU.add))
            dve.tensor_copy(slot[:], slot_f[:]).then_inc(slots_ready, 1)
            link(dve.tensor_tensor(ended[:], ends[:, PAD_E:].unsqueeze(1).broadcast_to([P, SLOTS + AHEAD, NE]),
                                   tile_nos[:].unsqueeze(2).broadcast_to([P, SLOTS + AHEAD, NE]), ALU.is_le))
            link(dve.tensor_reduce(expert_f[:], ended[:], AX.X, ALU.add))
            link(dve.tensor_scalar(expert_f[:], expert_f[:], float(NE - 1), None, ALU.min))
            dve.tensor_copy(tile_expert[:], expert_f[:]).then_inc(chosen_known, 1)

            for n in range(1, 2 * NE, 2):
                dve.wait_ge(w_turned, n + 1)
                dve.tensor_copy(experts[:, n // 2, FF:2 * FF],
                                ps_five[:, n % 4, :]).then_inc(w_by_dve, 1)
            dve.wait_ge(w_by_act, NE)
            dve.wait_ge(w_by_dve, NE)
            dve.wait_ge(w_turned, 2 * NE)
            dve.wait_ge(chosen_known, 1)

            def copy_expert(i, slot_no):
                expert = dve.value_load(tile_expert[0:1, bass.ds(i, 1)], min_val=0, max_val=NE - 1)
                dve.tensor_copy(chosen[:, slot_no:slot_no + 1, :],
                                experts[:, bass.ds(expert, 1), :]).then_inc(expert_copied, 1)

            for i in range(AHEAD):
                copy_expert(i, i)
            with dve.Fori(0, ROUNDS) as rnd:
                for k in range(BODY):
                    dve.wait_ge(y_taken, rnd * BODY + k + PRIMED)
                    copy_expert(rnd * BODY + k + AHEAD, (k + AHEAD) % 4)
                    dve.wait_ge(y_full, rnd * BODY + k + 1 + PRIMED)
                    dve.wait_ge(y_stored[k % 4], rnd * (16 * BODY // 4) + 16 * (k // 4) + PRIMED)
                    dve.tensor_tensor(tile_y[:, k % 4, :], ps_five[:, 2 + k % 2, 0:E],
                                      chosen[:, k % 4, 2 * FF + FT:EXPERT], ALU.add).then_inc(y_taken, 1)

            for c in range(NC):
                dve.wait_ge(gathered[c], 16 * TPC)
                part = y_back[:, TPC * c:TPC * c + TPC, :]
                link(dve.tensor_tensor(part, part, gate_b[:].unsqueeze(1).broadcast_to([P, TPC, E]), ALU.mult))
                dve.tensor_tensor(part, part, x_sb[:, TPC * c:TPC * c + TPC, :], ALU.add).then_inc(out_ready, 1)


_INS = ['L0_attn_x', 'L0_attn_w_qkv', 'L0_attn_w_out', 'L0_ffn_Wr', 'L0_ffn_br', 'L0_ffn_W1', 'L0_ffn_b1',
        'L0_ffn_W2', 'L0_ffn_b2', 'L0_c', 'L0_wmod']
_OUTS = [((1, 2048, 128), 'float32')]


def kernel(**inputs):
    import numpy as _np
    import concourse.bacc as _bacc
    from concourse import mybir as _mybir
    from concourse.bass_utils import run_bass_kernel_spmd as _run

    nc = _bacc.Bacc("TRN2", target_bir_lowering=False, num_devices=1)
    arrays, args = {}, []
    for name in _INS:
        a = _np.ascontiguousarray(inputs[name])
        arrays[f"in_{name}_dram"] = a
        args.append(nc.dram_tensor(f"in_{name}_dram", a.shape, _mybir.dt.from_np(a.dtype), kind="ExternalInput").ap())
    for i, (shape, dtype) in enumerate(_OUTS):
        dt = _mybir.dt.from_np(_np.dtype(dtype))
        args.append(nc.dram_tensor(f"out_{i}_dram", shape, dt, kind="ExternalOutput").ap())
    adaln_block(nc, *args)
    r = _run(nc, [arrays], core_ids=[0])
    got = tuple(r.results[0][f"out_{i}_dram"] for i in range(len(_OUTS)))
    return got[0]
```

```python
from collections import namedtuple
from contextlib import ExitStack

import concourse.bass as bass
from concourse import mybir

ALU = mybir.AluOpType
ACT = mybir.ActivationFunctionType
AX = mybir.AxisListType
F32 = mybir.dt.float32
F32R = mybir.dt.float32r
I32 = mybir.dt.int32

P = 128
BANK = 512
RING = 4
TURN_BANKS = 3
TURN_BY_ACT = (True, True, False)
QG = 256
PV_LAG = 2
NEXT_CHUNKS = 2
SCORES_AT = [(0.05, 1.23), (0.95, 1.69), (2.05, 2.8), (2.9, 3.65),
             (4.15, 4.68), (4.95, 5.73), (6.0, 6.7)]
PROJ_AT = [(7.03, 7.18, 7.58), (7.84, 7.84, 7.84),
           (2.08, 2.4, 2.57), (4.03, 4.4, 4.67)]
NEXT_SCORES_AT = (7.9, 7.95, 8.0, 8.1)
OUT_AT = (3.4, 4.4, 6.7, 9.0)
EXP_LAG = [3, 2, 1, 3, 3, 4, 3, 2]
BACK_LAG = 0.35
WEIGHTS_FIRST = 5
LN_EPS = 1e-5
MASKED = -2.38e38
LOWEST = -3.4e38
PRIMED = 1
MOD_MIN = 0.25

Step = namedtuple("Step", "kind own g h r j c bank use n")


def plan_pairs(S):
    groups = S // QG
    used, counts = [0] * RING, {}
    waiting, steps = [], []
    taken = [0]

    def emit(kind, own=0, g=0, h=0, r=0, j=0, c=0):
        bank = use = 0
        if kind in ("proj", "vproj", "score", "bcast", "out", "back"):
            bank = taken[0] % RING
            taken[0] += 1
            use = used[bank]
            used[bank] += 1
        n = counts.get((kind, own), 0)
        counts[kind, own] = n + 1
        steps.append(Step(kind, own, g, h, r, j, c, bank, use, n))

    def finish_row():
        own, g, r, _ = waiting.pop(0)
        emit("exp", own=own, g=g, h=r % 2, r=r)
        if r == 3:
            emit("sum", own=own, g=g)

    def run(items):
        for kind, at in items:
            while kind == "turn" and waiting and waiting[0][1] == at["g"]:
                finish_row()
            emit(kind, **at)
            if kind == "score" and at["c"] == chunks(at["g"]) - 1:
                waiting.append((at.get("own", 0), at["g"], at["r"], len(steps)))
            while waiting and len(steps) - waiting[0][3] >= EXP_LAG[waiting[0][1]]:
                finish_row()
        while waiting:
            finish_row()

    def project(c, own=0):
        return [("proj", dict(own=own, j=j, c=c)) for j in range(2)] + [("vproj", dict(own=own, c=c))]

    def scores(g, own=0):
        return [("score", dict(own=own, g=g, h=r % 2, r=r, c=c)) for r in range(4) for c in range(chunks(g))]

    run(project(0) + project(1) + scores(0))
    before, before_used, before_counts = list(steps), list(used), dict(counts)

    timed, late = [], []
    for g in range(groups):
        tiles = 2 * g + 2
        for j in range(tiles):
            now = g + (j + 0.5) / tiles
            if len(late) > PV_LAG:
                timed += [(now, item) for item in late.pop(0)]
            timed.append((now, ("turn", dict(g=g, j=j))))
            if j == 1:
                timed.append((now, ("bcast", dict(g=g))))
            late.append([("pv", dict(g=g, j=j))] + ([("norm", dict(g=g))] if j == tiles - 1 else []))
    for i, items in enumerate(late):
        timed += [(groups + 0.05 * i, item) for item in items]
    timed += [(at, ("out", dict(c=c))) for c, at in enumerate(OUT_AT)]
    for g in range(1, groups):
        ahead, (start, end) = scores(g), SCORES_AT[g - 1]
        timed += [(start + (end - start) * (i + 0.5) / len(ahead), item) for i, item in enumerate(ahead)]
    for c in range(S // BANK):
        timed += zip(PROJ_AT[c], project(c, own=1 if c < NEXT_CHUNKS else 0))
    timed += zip(NEXT_SCORES_AT, scores(0, own=1))
    order = [item for _, item in sorted(timed, key=lambda entry: entry[0])]

    def one_pair(items):
        steps.clear()
        taken[0] = 0
        used[:] = before_used
        counts.clear()
        counts.update(before_counts)
        run(items)
        return list(steps)

    turn = one_pair(order)
    uses = [a - b for a, b in zip(used, before_used)]
    timed += [(at, (kind, dict(c=c))) for c, at in enumerate(OUT_AT) for kind, at in
              (("gate", at + 0.001), ("back", at + BACK_LAG))]
    timed = [entry for entry in timed if not entry[1][1].get("own", 0)]
    last = one_pair([item for _, item in sorted(timed, key=lambda entry: entry[0])])
    totals = {kind: n for (kind, own), n in counts.items() if not own}
    return before, turn, last, uses, list(used), totals


def piece(g, r, c):
    tiles = 2 * g + r // 2 + 1
    starts = list(range(0, tiles, BANK // P)) + [tiles]
    if tiles > 1 and tiles % (BANK // P) == 1:
        starts[-2] -= 1
    return starts[c] * P, (starts[c + 1] - starts[c]) * P


def chunks(g):
    return (2 * g + 2 + 3) // 4


def adaln_block(nc, x, w_qkv, w_out, Wr, br, W1, b1, W2, b2, c_in, wmod, out):
    _, S, E = x.shape
    _, H, D3 = w_qkv.shape
    D = D3 // 3
    NE, FF, _ = W1.shape
    T = S // P
    NC = S // BANK
    TPC = BANK // P
    FT = FF // P
    PAIRS = H // 2
    GROUPS = S // QG
    Q_SCALE = float(D) ** -0.5
    BODY = 12
    ROUNDS = -(-(T + NE - 1) // BODY)
    SLOTS = ROUNDS * BODY
    CHOSEN = 4
    LOADED = 5
    LOADS = 6
    ROW = E + 1
    IN_SLOTS = 12
    EXPERT = 2 * FF + FT + E
    assert E == P and D == 64 and Q_SCALE == 0.125 and FF == BANK

    before, steps, last, uses, last_used, counts = plan_pairs(S)
    ring_tail = [n + (PAIRS - 1) * u for n, u in zip(last_used, uses)]

    with ExitStack() as ctx:
        def sb(name, shape, dt=F32):
            return ctx.enter_context(nc.sbuf_tensor(name, shape, dt))

        def sem(name):
            return ctx.enter_context(nc.semaphore(name))

        x_sb = sb("x_sb", [P, T, E])
        hT = sb("hT", [P, S])
        q_split = [sb(f"q_split{h}", [P, S], F32R) for h in range(2)]
        k_split = [sb(f"k_split{h}", [P, 2, S], F32R) for h in range(2)]
        v_sb = sb("v_sb", [P, T, P])
        w_pair = sb("w_pair", [P, 3, 2 * D])
        wo_pair = sb("wo_pair", [P, E])
        probs = sb("probs", [P, 2, 4, S])
        pT = sb("pT", [P, TURN_BANKS, BANK])
        rinv_b = sb("rinv_b", [P, 2, QG])
        oT = sb("oT", [P, S])
        accT = sb("accT", [P, S])
        row_max = sb("row_max", [P, GROUPS, 4, 4])
        neg_max = sb("neg_max", [P, GROUPS, 4])
        row_sum = sb("row_sum", [P, GROUPS, 4])
        rinv = sb("rinv", [P, GROUPS, 4])
        rinv_hi = sb("rinv_hi", [P, 2, 4, D], F32R)
        rinv_lo = sb("rinv_lo", [P, 2, 4, D], F32R)
        ident = sb("ident", [P, P])
        ident_r = sb("ident_r", [P, P], F32R)
        causal = sb("causal", [P, BANK])
        w1_rows = sb("w1_rows", [P, NE * FT, E])
        after = probs[:].rearrange("p a r s -> p (a r s)")
        experts = after[:, 0:NE * EXPERT].rearrange("p (e c) -> p e c", e=NE)
        w2_rows = after[:, NE * EXPERT:NE * EXPERT + NE * FF].rearrange(
            "p (e f) -> p e f", e=NE)
        chosen = after[:, NE * EXPERT:(NE + CHOSEN) * EXPERT].rearrange(
            "p (s c) -> p s c", s=CHOSEN)
        rows = after[:, (NE + CHOSEN) * EXPERT:(NE + CHOSEN) * EXPERT + T * ROW].rearrange(
            "p (t c) -> p t c", t=T)
        token_nos = sb("token_nos", [P, T], I32)
        b1_rows = sb("b1_rows", [NE * FT, P])
        wr_rows = sb("wr_rows", [NE, E])
        wrT = sb("wrT", [P, NE])
        br_b = sb("br_b", [P, NE])
        c_col = sb("c_col", [P, 1])
        c_exp = sb("c_exp", [P, 1])
        c_den = sb("c_den", [P, 1])
        c_rec = sb("c_rec", [P, 1])
        c_silu = sb("c_silu", [P, 1])
        wmod_sb = probs[:, 1, 3, 0:6 * E]
        mod = sb("mod", [P, 8])
        ga_sign = sb("ga_sign", [P, 1])
        ga_size = sb("ga_size", [P, 1])
        gate_a = sb("gate_a", [P, 1])
        gb_raw = sb("gb_raw", [P, E])
        gb_sign = sb("gb_sign", [P, E])
        gb_size = sb("gb_size", [P, E])
        gate_b = sb("gate_b", [P, E])
        stats = sb("stats", [P, T, 6])
        mean_var = sb("mean_var", [P, T, 2])
        var_eps = sb("var_eps", [P, T])
        std = sb("std", [P, T])
        rough = sb("rough", [P, T])
        newton = sb("newton", [P, T])
        rstd = sb("rstd", [P, T])
        logits = sb("logits", [P, T, NE])
        top = sb("top", [P, T])
        is_top = sb("is_top", [P, T, NE])
        expert_no = sb("expert_no", [P, NE])
        top_no = sb("top_no", [P, T, NE])
        first_no = sb("first_no", [P, T])
        onehot = sb("onehot", [P, T, NE])
        PAD_T, PAD_E = T // 2, NE // 2
        upto_t = [sb(f"upto_t{i}", [P, PAD_T + T, NE]) for i in range(2)]
        upto_e = [sb(f"upto_e{i}", [P, PAD_E + NE]) for i in range(2)]
        steps_of_p = sb("steps_of_p", [P, T])
        above = sb("above", [P, NE, T])
        slot_parts = sb("slot_parts", [P, T, NE])
        slot_f = sb("slot_f", [P, T])
        slot = sb("slot", [P, T], I32)
        tile_nos = sb("tile_nos", [P, SLOTS + CHOSEN])
        ended = sb("ended", [P, SLOTS + CHOSEN, NE])
        expert_f = sb("expert_f", [P, SLOTS + CHOSEN])
        tile_expert = sb("tile_expert", [P, SLOTS + CHOSEN], I32)
        earlier = sb("earlier", [P, P])
        ones = sb("ones", [P, P])
        zeros = sb("zeros", [P, E])
        spare_nos = sb("spare_nos", [P, SLOTS + LOADED, 1], I32)
        x_sorted = nc.dram_tensor("x_sorted", [(SLOTS + LOADED) * P, ROW], F32).ap()
        y_rows = nc.dram_tensor("y_rows", [S + (SLOTS + LOADED) * P, E], F32).ap()

        ps = ctx.enter_context(nc.psum_tensor("ps", [P, 8, BANK], F32))
        ps_ring = ps[:, 0:RING, :]
        ps_turn = ps[:, RING:RING + TURN_BANKS, :]
        ps_o = ps[:, 7, :]
        ps_five = ps[:, 0:5, :]
        ps_two = ps[:, 5:7, :]

        x_in = [sem(f"x_in{c}") for c in range(NC)]
        mod_in = sem("mod_in")
        late_in = sem("late_in")
        w2_in = sem("w2_in")
        small_turned = sem("small_turned")
        small_ready = sem("small_ready")
        ident_made = sem("ident_made")
        ident_cast = sem("ident_cast")
        dve_chain = sem("dve_chain")
        c_exp_done = sem("c_exp_done")
        silu_done = sem("silu_done")
        mod_full = sem("mod_full")
        mod_done = sem("mod_done")
        var_ready = sem("var_ready")
        sqrt_done = sem("sqrt_done")
        norm_ready = sem("norm_ready")
        turn_full = sem("turn_full")
        h_ready = sem("h_ready")
        acc_zeroed = sem("acc_zeroed")
        w_in = sem("w_in")
        wo_in = sem("wo_in")
        bank_full = [sem(f"bank_full{b}") for b in range(RING)]
        bank_free = [sem(f"bank_free{b}") for b in range(RING)]
        hi_ready = sem("hi_ready")
        k_doubled = [sem(f"k_doubled{c}") for c in range(NC)]
        negmax_ready = sem("negmax_ready")
        masks_begun = sem("masks_begun")
        sums_step = sem("sums_step")
        rinv_ready = sem("rinv_ready")
        pT_full = sem("pT_full")
        exp_done = sem("exp_done")
        pT_taken = [sem(f"pT_taken{b}") for b in range(TURN_BANKS)]
        pv_done = sem("pv_done")
        o_ready = sem("o_ready")
        gated = sem("gated")
        w_turned = sem("w_turned")
        w_copied = sem("w_copied")
        logits_full = sem("logits_full")
        onehot_ready = sem("onehot_ready")
        sort_full = sem("sort_full")
        slots_ready = sem("slots_ready")
        chosen_known = sem("chosen_known")
        numbered = sem("numbered")
        scattered = sem("scattered")
        zero_made = sem("zero_made")
        zero_stored = sem("zero_stored")
        tile_read = [sem(f"tile_read{k}") for k in range(LOADS)]
        tile_turned = sem("tile_turned")
        loads_begun = sem("loads_begun")
        tile_h_ready = sem("tile_h_ready")
        expert_copied = sem("expert_copied")
        hid_full = sem("hid_full")
        hid_ready = sem("hid_ready")
        y_full = sem("y_full")
        y_taken = sem("y_taken")
        stores_begun = sem("stores_begun")
        y_stored = [sem(f"y_stored{k}") for k in range(4)]
        y_in = [sem(f"y_in{c}") for c in range(NC)]
        out_ready = sem("out_ready")
        out_stored = sem("out_stored")

        x_tiles = x.rearrange("a (t p) e -> p (a t) e", p=P)
        out_tiles = out.rearrange("a (t p) e -> p (a t) e", p=P)
        w_qkv_pairs = w_qkv.rearrange("e (n h) d -> n e h d", h=2)
        w_out_pairs = w_out.rearrange("(n h) d e -> n (h d) e", h=2)
        tile_in = hT[:, 0:IN_SLOTS * ROW].rearrange("p (s c) -> p s c", s=IN_SLOTS)
        tile_hT = v_sb[:, 0:2, :]
        tile_y = v_sb[:, 4:8, :]
        hidT = oT[:].rearrange("p (s f n) -> p s f n", s=4, f=FT)
        y_back = accT[:].rearrange("p (t d) -> p t d", t=T)
        x_sorted_rows = x_sorted.rearrange("(i p) d -> p i d", p=P)
        x_sorted_tiles = x_sorted.rearrange("(i p) d -> i p d", p=P)
        y_tiles = y_rows[0:S, :].rearrange("(t p) d -> p t d", p=P)

        def stored(k):
            return 16 * (k // 4 + 1) + 16

        def own_half(h):
            return slice(D * h, D * h + D)

        block = ctx.enter_context(nc.Block())

        @block.sync
        def _(sp):
            def load_pair(pair):
                for j in range(3):
                    sp.dma_start(w_pair[:, j, :].rearrange("e (h d) -> e h d", h=2),
                                 w_qkv_pairs[pair, :, :, j * D:(j + 1) * D]).then_inc(w_in, 16)

            for c in range(NC):
                sp.dma_start(x_sb[:, TPC * c:TPC * c + TPC, :],
                             x_tiles[:, TPC * c:TPC * c + TPC, :]).then_inc(x_in[c], 16)
                if c == 0:
                    sp.dma_start(c_col[:], c_in.rearrange("a e -> e a")).then_inc(mod_in, 16)
                    sp.dma_start(wmod_sb, wmod).then_inc(mod_in, 16)
            load_pair(0)
            sp.dma_start(wo_pair[:], w_out_pairs[0]).then_inc(wo_in, 16)
            sp.dma_start(w1_rows[:], W1.rearrange("e (f p) d -> p (e f) d", p=P)).then_inc(late_in, 16)
            sp.dma_start(b1_rows[:], b1.rearrange("e (f p) -> (e f) p", p=P)).then_inc(late_in, 16)
            sp.dma_start(wr_rows[:], Wr).then_inc(late_in, 16)
            sp.wait_ge(zero_made, 2)
            sp.dma_start(x_sorted_rows[:, :, 0:E],
                         zeros[:].unsqueeze(1).broadcast_to([P, SLOTS + LOADED, E])).then_inc(zero_stored, 16)
            sp.dma_start(x_sorted_rows[:, :, E:ROW].bitcast(I32), spare_nos[:],
                         allow_slow_non_contiguous=True).then_inc(zero_stored, 16)
            sp.dma_start(br_b[:], br.rearrange("(a n) -> a n", a=1).broadcast_to([P, NE])).then_inc(late_in, 16)

            def serve(pair, steps, next_pair):
                for s in steps:
                    done = pair * uses[s.bank] + s.use + 1 + PRIMED
                    if s.kind == "proj" and s.j == 1:
                        sp.wait_ge(bank_free[s.bank], done)
                        cols = slice(s.c * BANK, (s.c + 1) * BANK)
                        for h in range(2):
                            sp.dma_start(k_split[h][own_half(1 - h), :, cols].bitcast(F32),
                                         k_split[h][own_half(h), :, cols].bitcast(F32)).then_inc(k_doubled[s.c], 16)
                    elif s.kind == "vproj" and s.c == NC - 1 and next_pair is not None:
                        sp.wait_ge(bank_free[s.bank], done)
                        load_pair(next_pair)
                    elif s.kind == "out" and s.c == NC - 1 and next_pair is not None:
                        sp.wait_ge(bank_free[s.bank], done)
                        sp.dma_start(wo_pair[:], w_out_pairs[next_pair]).then_inc(wo_in, 16)

            serve(0, before, None)
            with sp.Fori(0, PAIRS - 1) as pair:
                serve(pair, steps, pair + 1)
            serve(PAIRS - 1, last, None)
            for c in range(NC):
                sp.wait_ge(k_doubled[c], 32 * PAIRS)
            sp.wait_ge(pT_full, PAIRS * counts["turn"] + PRIMED)
            sp.dma_start(w2_rows, W2.rearrange("e d f -> d e f")).then_inc(w2_in, 16)
            sp.dma_start(experts[:, :, 2 * FF + FT:EXPERT],
                         b2.rearrange("(a e) d -> a e d", a=1).broadcast_to([P, NE, E])).then_inc(w2_in, 16)
            sp.wait_ge(scattered, 16 * T)
            for k in range(LOADED):
                sp.dma_start(tile_in[:, k, :], x_sorted_tiles[k]).then_inc(tile_read[k], 16)
            with sp.Fori(0, ROUNDS) as rnd:
                for k in range(BODY):
                    sp.wait_ge(tile_turned, rnd * BODY + k + 1)
                    sp.sem_inc(loads_begun, 1)
                    old = k + LOADED - IN_SLOTS
                    old = old if old >= -4 else old + 4
                    sp.wait_ge(y_stored[old % 4], rnd * (16 * BODY // 4) + stored(old))
                    sp.dma_start(tile_in[:, (k + LOADED) % IN_SLOTS, :], x_sorted_tiles[rnd * BODY + k + LOADED]
                                 ).then_inc(tile_read[(k + LOADED) % LOADS], 16)
            for k in range(4):
                sp.wait_ge(y_stored[k], 16 * (SLOTS // 4) + 16)
            for c in range(NC):
                sp.dma_start(y_back[:, TPC * c:TPC * c + TPC, :],
                             y_tiles[:, TPC * c:TPC * c + TPC, :]).then_inc(y_in[c], 16)
            for c in range(NC):
                sp.wait_ge(out_ready, c + 1)
                sp.dma_start(out_tiles[:, TPC * c:TPC * c + TPC, :],
                             y_back[:, TPC * c:TPC * c + TPC, :]).then_inc(out_stored, 16)
            for k in range(LOADS):
                sp.wait_ge(tile_read[k], 16 * (SLOTS // LOADS + (1 if k < LOADED else 0)))
            sp.wait_ge(out_stored, 16 * NC)

        @block.gpsimd
        def _(pool):
            nc.gpsimd.memset(ident[:], 0.0).then_inc(ident_made, 1)
            nc.gpsimd.memset(causal[:], 0.0).then_inc(ident_made, 1)
            nc.gpsimd.iota(expert_no[:], pattern=[[1, NE]], base=-NE, channel_multiplier=0,
                           allow_small_or_imprecise_dtypes=True).then_inc(ident_made, 1)
            nc.gpsimd.iota(steps_of_p[:], pattern=[[P, T]], base=0, channel_multiplier=0,
                           allow_small_or_imprecise_dtypes=True).then_inc(ident_made, 1)
            nc.gpsimd.iota(tile_nos[:], pattern=[[1, SLOTS + CHOSEN]], base=0, channel_multiplier=0,
                           allow_small_or_imprecise_dtypes=True).then_inc(ident_made, 1)
            nc.gpsimd.memset(ones[:], 1.0).then_inc(ident_made, 1)
            pool.wait_ge(ident_made, 6)
            nc.gpsimd.affine_select(out=ident[:], in_=ident[:], compare_op=ALU.not_equal, fill=1.0,
                                    base=0, pattern=[[-1, P]], channel_multiplier=1).then_inc(ident_made, 1)
            nc.gpsimd.affine_select(out=causal[:, BANK - P:], in_=causal[:, BANK - P:], compare_op=ALU.is_ge, fill=MASKED,
                                    base=0, pattern=[[-1, P]], channel_multiplier=1).then_inc(ident_made, 1)
            nc.gpsimd.affine_select(out=earlier[:], in_=ones[:], compare_op=ALU.is_ge, fill=0.0,
                                    base=-1, pattern=[[1, P]], channel_multiplier=-1).then_inc(ident_made, 1)
            nc.gpsimd.iota(token_nos[:], pattern=[[P, T]], base=0, channel_multiplier=1,
                           allow_small_or_imprecise_dtypes=True).then_inc(ident_made, 1)
            nc.gpsimd.memset(zeros[:], 0.0).then_inc(zero_made, 1)
            nc.gpsimd.iota(spare_nos[:], pattern=[[P, SLOTS + LOADED], [0, 1]], base=S, channel_multiplier=1,
                           allow_small_or_imprecise_dtypes=True).then_inc(zero_made, 1)
            pool.wait_ge(zero_made, 2)

            for k in range(4):
                pool.dma_start(y_rows[S + k:S + k + 1, :], zeros[0:1, :]).then_inc(y_stored[k], 16)
            for k in range(4):
                pool.wait_ge(y_stored[k], 16)
            pool.wait_ge(numbered, 1)
            pool.wait_ge(slots_ready, 1)
            pool.wait_ge(zero_stored, 32)
            for t in range(T):
                pool.indirect_dma_start(x_sorted, bass.IndirectOffsetOnAxis(slot[:, t:t + 1], 0),
                                        rows[:, t, :], None).then_inc(scattered, 16)
            with pool.Fori(0, ROUNDS) as rnd:
                for k in range(BODY):
                    pool.wait_ge(y_taken, rnd * BODY + k + 1 + PRIMED)
                    pool.sem_inc(stores_begun, 1)
                    numbers = tile_in[:, k % IN_SLOTS, E:ROW].bitcast(I32)
                    pool.indirect_dma_start(y_rows, bass.IndirectOffsetOnAxis(numbers, 0),
                                            tile_y[:, k % 4, :], None).then_inc(y_stored[k % 4], 16)

        @block.tensor
        def _(pe):
            for primed in (pT_full, pv_done, hid_full, y_full):
                pe.sem_inc(primed, PRIMED)
            pe.wait_ge(silu_done, 1)
            for j in range(6):
                pe.matmul(ps_o[:, j:j + 1], wmod_sb[:, E * j:E * j + E], c_silu[:], start=True, stop=True)
            pe.matmul(ps_o[:, E:2 * E], c_silu[:].to_broadcast([P, P]), wmod_sb[:, 5 * E:6 * E],
                      start=True, stop=True).then_inc(mod_full, 1)

            def turn_tokens(base, tiles):
                for c in range(NC):
                    pe.wait_ge(norm_ready, base + c + 1)
                    if c >= 2:
                        pe.wait_ge(h_ready, base + c - 1)
                    for t in range(TPC):
                        m = pe.transpose(ps_two[:, c % 2, P * t:P * t + P], tiles[:, TPC * c + t, 0:E], ident[:])
                    m.then_inc(turn_full, 1)

            pe.wait_ge(ident_made, 9)
            turn_tokens(0, y_back)
            pe.wait_ge(ident_cast, 1)
            pe.wait_ge(h_ready, NC)
            turns_per_bank = counts["turn"] // TURN_BANKS

            def run(pair, steps):
                def free(s):
                    pe.wait_ge(bank_free[s.bank], pair * uses[s.bank] + s.use + PRIMED)

                v_projected = {(s.own, s.c): s for s in steps if s.kind == "vproj"}
                for s in steps:
                    if s.kind == "proj":
                        if s.c == 0:
                            pe.wait_ge(w_in, pair * 48 + s.own * 48 + 48)
                        free(s)
                        pe.matmul(ps_ring[:, s.bank, :], w_pair[:, s.j, :], hT[:, s.c * BANK:(s.c + 1) * BANK],
                                  start=True, stop=True).then_inc(bank_full[s.bank], 1)
                    elif s.kind == "vproj":
                        free(s)
                        for t in range(TPC):
                            m = pe.matmul(ps_ring[:, s.bank, P * t:P * t + P],
                                          hT[:, (TPC * s.c + t) * P:(TPC * s.c + t + 1) * P],
                                          w_pair[:, 2, :], start=True, stop=True)
                        m.then_inc(bank_full[s.bank], 1)
                    elif s.kind == "score":
                        if s.g % 2 == 0 and s.r == 0 and s.c == 0:
                            pe.wait_ge(k_doubled[s.g // 2], pair * 32 + 32 * s.own + 32)
                        free(s)
                        k0, w = piece(s.g, s.r, s.c)
                        w = max(w, 2 * P)
                        q0 = (2 * s.g + s.r // 2) * P
                        q = q_split[s.h][:, q0:q0 + P]
                        keys = slice(k0, k0 + w)
                        for part in range(2):
                            m = pe.matmul(ps_ring[:, s.bank, 0:w], q, k_split[s.h][:, part, keys],
                                          start=(part == 0), stop=(part == 1))
                        m.then_inc(bank_full[s.bank], 1)
                    elif s.kind == "turn":
                        if s.j == 0:
                            pe.wait_ge(exp_done, pair * (4 * GROUPS) + 4 * s.g + 4)
                        bank = s.n % TURN_BANKS
                        pe.wait_ge(pT_taken[bank], pair * turns_per_bank + s.n // TURN_BANKS + PRIMED)
                        for r in range(0 if s.j <= 2 * s.g else 2, 4):
                            m = pe.transpose(ps_turn[:, bank, P * r:P * r + P],
                                             probs[:, s.g % 2, r, s.j * P:s.j * P + P], ident[:])
                        m.then_inc(pT_full, 1)
                    elif s.kind == "bcast":
                        pe.wait_ge(rinv_ready, pair * GROUPS + s.g + 1)
                        free(s)
                        for u in range(2):
                            for part in (rinv_hi, rinv_lo):
                                m = pe.matmul(ps_ring[:, s.bank, P * u:P * u + P],
                                              part[:, s.g % 2, 2 * u:2 * u + 2, :].rearrange("p h d -> p (h d)"),
                                              ident_r[:], start=part is rinv_hi, stop=part is rinv_lo)
                        m.then_inc(bank_full[s.bank], 1)
                    elif s.kind == "pv":
                        if s.j == 0:
                            pe.wait_ge(o_ready, pair * GROUPS + s.g + PRIMED)
                            if s.g % 2 == 0 and s.g // 2 >= NEXT_CHUNKS:
                                v = v_projected[0, s.g // 2]
                                pe.wait_ge(bank_free[v.bank], pair * uses[v.bank] + v.use + 1 + PRIMED)
                        bank = s.n % TURN_BANKS
                        pe.wait_ge(pT_taken[bank], pair * turns_per_bank + s.n // TURN_BANKS + 1 + PRIMED)
                        u0 = 0 if s.j <= 2 * s.g else 1
                        turned = pT[:, bank, :].rearrange("p (u h i) -> p u h i", u=2, h=2)
                        for h in range(2):
                            m = pe.matmul(ps_o[D * h:D * h + D, P * u0:QG], v_sb[:, s.j, D * h:D * h + D],
                                          turned[:, u0:2, h, :], start=(s.j == 0), stop=(s.j == 2 * s.g + 1),
                                          skip_group_check=True)
                        m.then_inc(pv_done, 1)
                    elif s.kind == "out":
                        if s.n == 0:
                            pe.wait_ge(wo_in, pair * 16 + 16)
                        pe.wait_ge(o_ready, pair * GROUPS + 2 * s.c + 2 + PRIMED)
                        free(s)
                        pe.matmul(ps_ring[:, s.bank, :], wo_pair[:], oT[:, s.c * BANK:(s.c + 1) * BANK],
                                  start=True, stop=True).then_inc(bank_full[s.bank], 1)
                    elif s.kind == "back":
                        pe.wait_ge(gated, s.c + 1)
                        free(s)
                        for t in range(TPC):
                            m = pe.transpose(ps_ring[:, s.bank, P * t:P * t + P],
                                             oT[:, (TPC * s.c + t) * P:(TPC * s.c + t + 1) * P], ident[:])
                        m.then_inc(bank_full[s.bank], 1)

            run(0, before)
            with pe.Fori(0, PAIRS - 1) as pair:
                run(pair, steps)
            run(PAIRS - 1, last)

            pe.wait_ge(late_in, 16 * 4)
            pe.transpose(ps_five[:, 4, 0:NE * FT], b1_rows[:], ident[0:NE * FT, 0:NE * FT])
            pe.transpose(ps_five[:, 4, NE * FT:NE * FT + NE], wr_rows[:], ident[0:NE, 0:NE]).then_inc(small_turned, 1)

            for b in range(RING):
                pe.wait_ge(bank_free[b], ring_tail[b] + PRIMED)
            def turn_weights(first, end):
                for n in range(first, end):
                    if n == NE:
                        pe.wait_ge(w2_in, 32)
                    if n >= 4:
                        pe.wait_ge(w_copied, n - 3)
                    for f in range(FT):
                        e = n % NE
                        w_rows = w1_rows[:, e * FT + f, :] if n < NE else w2_rows[:, e, f * P:(f + 1) * P]
                        m = pe.transpose(ps_five[:, n % 4, P * f:P * f + P], w_rows, ident[:])
                    m.then_inc(w_turned, 1)

            turn_weights(0, WEIGHTS_FIRST)
            turn_tokens(NC, rows)
            pe.wait_ge(h_ready, 2 * NC)
            pe.wait_ge(small_ready, 1)
            for t in range(T):
                m = pe.matmul(ps_o[:, t * NE:t * NE + NE], hT[:, t * P:t * P + P], wrT[:], start=True, stop=True)
            m.then_inc(logits_full, 1)

            pe.wait_ge(onehot_ready, 1)
            flat = onehot[:].rearrange("p t n -> p (t n)")
            pe.matmul(ps_two[:, 0, 0:T * NE], earlier[:], flat, start=True, stop=True)
            pe.matmul(ps_two[:, 1, 0:T * NE], ones[:], flat, start=True, stop=True).then_inc(sort_full, 1)
            turn_weights(WEIGHTS_FIRST, 2 * NE)

            def turn_tile(k):
                pe.transpose(ps_two[:, k % 2, 0:P], tile_in[:, k % IN_SLOTS, 0:E], ident[:]).then_inc(tile_turned, 1)

            pe.wait_ge(tile_read[0], 16)
            turn_tile(0)
            with pe.Fori(0, ROUNDS) as rnd:
                def turn(k):
                    pe.wait_ge(tile_read[k % LOADS], rnd * (16 * BODY // LOADS) + 16 * (k // LOADS) + 16)
                    pe.wait_ge(tile_h_ready, rnd * BODY + k - 1 + PRIMED)
                    turn_tile(k)

                def hidden(k):
                    pe.wait_ge(tile_h_ready, rnd * BODY + k + 1 + PRIMED)
                    pe.wait_ge(expert_copied, rnd * BODY + k + 1)
                    pe.wait_ge(hid_ready, rnd * BODY + max(0, k - 1) + PRIMED)
                    for f in range(FT):
                        m = pe.matmul(ps_five[:, k % 2, f * P:(f + 1) * P], chosen[:, k % CHOSEN, f * P:(f + 1) * P],
                                      tile_hT[:, k % 2, :], start=True, stop=True)
                    m.then_inc(hid_full, 1)

                def output(k):
                    pe.wait_ge(hid_ready, rnd * BODY + k + 1 + PRIMED)
                    pe.wait_ge(y_taken, rnd * BODY + max(0, k - 1) + PRIMED)
                    for f in range(FT):
                        m = pe.matmul(ps_five[:, 2 + k % 2, 0:E], hidT[:, k % 4, f, :],
                                      chosen[:, k % CHOSEN, FF + f * E:FF + (f + 1) * E], start=(f == 0),
                                      stop=(f == FT - 1))
                    m.then_inc(y_full, 1)

                for k in range(BODY):
                    turn(k + 1)
                    hidden(k)
                    if k >= 2:
                        output(k - 2)
                output(BODY - 2)
                output(BODY - 1)

        @block.scalar
        def _(act):
            for primed in (tile_h_ready, hid_ready):
                act.sem_inc(primed, PRIMED)
            act.wait_ge(mod_in, 32)
            act.activation(c_exp[:], c_col[:], ACT.Exp, scale=-1.0).then_inc(c_exp_done, 1)

            def copy_weights(first, end):
                for n in range(first, end):
                    act.wait_ge(w_turned, n + 1)
                    at = 0 if n < NE else FF
                    act.copy(experts[:, n % NE, at:at + FF], ps_five[:, n % 4, :]).then_inc(w_copied, 1)

            def take_h(base, scale_col, bias_col):
                act.wait_ge(var_ready, base // NC + 1)
                act.activation(std[:], var_eps[:], ACT.Sqrt).then_inc(sqrt_done, 1)
                if base:
                    copy_weights(0, WEIGHTS_FIRST)
                act.wait_ge(mod_done, 1)
                for c in range(NC):
                    act.wait_ge(turn_full, base + c + 1)
                    act.activation(hT[:, c * BANK:(c + 1) * BANK], ps_two[:, c % 2, :], ACT.Identity,
                                   bias=mod[:, bias_col:bias_col + 1],
                                   scale=mod[:, scale_col:scale_col + 1]).then_inc(h_ready, 1)

            take_h(0, 6, 0)

            def run(pair, steps):
                def full(s):
                    act.wait_ge(bank_full[s.bank], pair * uses[s.bank] + s.use + 1)

                for s in steps:
                    if s.kind == "proj":
                        full(s)
                        for h in range(2):
                            dst = q_split[h] if s.j == 0 else k_split[h][:, 0, :]
                            m = act.mul(dst[own_half(h), s.c * BANK:(s.c + 1) * BANK],
                                        ps_ring[own_half(h), s.bank, :], Q_SCALE if s.j == 0 else 1.0)
                        m.then_inc(hi_ready, 1)
                    elif s.kind == "vproj":
                        full(s)
                        act.copy(v_sb[:, TPC * s.c:TPC * s.c + TPC, :].rearrange("p t d -> p (t d)"),
                                 ps_ring[:, s.bank, :]).then_inc(bank_free[s.bank], 1)
                    elif s.kind == "exp":
                        act.wait_ge(negmax_ready, pair * (4 * GROUPS) + 4 * (s.own * GROUPS + s.g) + s.r + 1)
                        keys = (2 * s.g + s.r // 2 + 1) * P
                        row = probs[:, s.g % 2, s.r, 0:keys]
                        act.activation(row, row, ACT.Exp, bias=neg_max[:, s.g, s.r:s.r + 1],
                                       accum_out=row_sum[:, s.g, s.r:s.r + 1]).then_inc(exp_done, 1)
                    elif s.kind == "turn" and TURN_BY_ACT[s.n % TURN_BANKS]:
                        bank = s.n % TURN_BANKS
                        act.wait_ge(pT_full, pair * counts["turn"] + s.n + 1 + PRIMED)
                        act.wait_ge(pv_done, pair * counts["pv"] + max(0, s.n - TURN_BANKS + 1) + PRIMED)
                        lo = 0 if s.j <= 2 * s.g else QG
                        act.copy(pT[:, bank, lo:BANK], ps_turn[:, bank, lo:BANK]).then_inc(pT_taken[bank], 1)
                    elif s.kind == "bcast":
                        full(s)
                        act.wait_ge(o_ready, pair * GROUPS + max(0, s.g - 1) + PRIMED)
                        act.copy(rinv_b[:, s.g % 2, :], ps_ring[:, s.bank, 0:QG]).then_inc(bank_free[s.bank], 1)
                    elif s.kind == "gate":
                        out_step = [o for o in steps if o.kind == "out" and o.c == s.c][0]
                        act.wait_ge(bank_free[out_step.bank],
                                    pair * uses[out_step.bank] + out_step.use + 1 + PRIMED)
                        cols = slice(s.c * BANK, (s.c + 1) * BANK)
                        act.mul(oT[:, cols], accT[:, cols], gate_a[:, 0:1]).then_inc(gated, 1)

            run(0, before)
            with act.Fori(0, PAIRS - 1) as pair:
                run(pair, steps)
            run(PAIRS - 1, last)

            take_h(NC, 7, 3)
            copy_weights(WEIGHTS_FIRST, 2 * NE)

            def modulate(k):
                act.activation(tile_hT[:, k % 2, :], ps_two[:, k % 2, 0:P], ACT.Identity,
                               bias=mod[:, 3:4], scale=mod[:, 7:8]).then_inc(tile_h_ready, 1)

            act.wait_ge(tile_turned, 1)
            modulate(0)
            with act.Fori(0, ROUNDS) as rnd:
                def rectify(k):
                    act.wait_ge(hid_full, rnd * BODY + k + 1 + PRIMED)
                    act.wait_ge(y_full, rnd * BODY + max(0, k - 3) + PRIMED)
                    for f in range(FT):
                        m = act.activation(hidT[:, k % 4, f, :], ps_five[:, k % 2, f * P:(f + 1) * P], ACT.Relu,
                                           bias=chosen[:, k % CHOSEN, 2 * FF + f:2 * FF + f + 1])
                    m.then_inc(hid_ready, 1)

                for k in range(BODY):
                    act.wait_ge(tile_turned, rnd * BODY + k + 2)
                    act.wait_ge(hid_full, rnd * BODY + k + PRIMED)
                    modulate(k + 1)
                    rectify(k)

        @block.vector
        def _(dve):
            chained = [0]

            def link(ins):
                chained[0] += 1
                ins.then_inc(dve_chain, 1)
                dve.wait_ge(dve_chain, chained[0])

            for primed in [o_ready, y_taken] + bank_free + pT_taken:
                dve.sem_inc(primed, PRIMED)
            dve.wait_ge(c_exp_done, 1)
            link(dve.tensor_scalar(c_den[:], c_exp[:], 1.0, None, ALU.add))
            link(dve.reciprocal(c_rec[:], c_den[:]))
            dve.tensor_tensor(c_silu[:], c_rec[:], c_col[:], ALU.mult).then_inc(silu_done, 1)

            def take_stats(tiles, loads=None):
                for t in tiles:
                    if loads and t % TPC == 0:
                        dve.wait_ge(loads[t // TPC], 16)
                    m = dve.bn_stats(stats[:, t, :], x_sb[:, t, :])
                link(m)
                for t in tiles:
                    m = dve.bn_aggr(mean_var[:, t, :], stats[:, t, :])
                link(m)

            def normalise(time, tiles):
                dve.tensor_scalar(var_eps[:], mean_var[:, :, 1], LN_EPS, None, ALU.add).then_inc(var_ready, 1)
                dve.wait_ge(var_ready, time + 1)
                dve.wait_ge(sqrt_done, time + 1)
                link(dve.reciprocal(rough[:], std[:]))
                link(dve.tensor_tensor(newton[:], rough[:], rough[:], ALU.mult))
                link(dve.tensor_tensor(newton[:], newton[:], var_eps[:], ALU.mult))
                link(dve.tensor_scalar(newton[:], newton[:], -0.5, 1.5, ALU.mult, ALU.add))
                link(dve.tensor_tensor(rstd[:], rough[:], newton[:], ALU.mult))
                for t in range(T):
                    m = dve.tensor_scalar(tiles[:, t, 0:E], x_sb[:, t, :], mean_var[:, t, 0:1],
                                          rstd[:, t:t + 1], ALU.subtract, ALU.mult)
                    if t % TPC == TPC - 1:
                        m.then_inc(norm_ready, 1)

            take_stats(range(T), x_in)
            normalise(0, y_back)
            dve.wait_ge(mod_full, 1)
            link(dve.tensor_copy(mod[:, 0:6], ps_o[:, 0:6]))
            dve.tensor_copy(gb_raw[:], ps_o[:, E:2 * E])
            dve.tensor_scalar(mod[:, 7:8], mod[:, 4:5], 1.0, None, ALU.add)
            link(dve.tensor_scalar(mod[:, 6:7], mod[:, 1:2], 1.0, None, ALU.add))
            gates = ((gate_a, ga_sign, ga_size, mod[:, 2:3]), (gate_b, gb_sign, gb_size, gb_raw[:]))
            for gate, sign, size, g in gates:
                m = dve.tensor_scalar(sign[:], g, 0.0, 2.0, ALU.is_ge, ALU.mult)
            link(m)
            for gate, sign, size, g in gates:
                m = dve.scalar_tensor_tensor(out=size[:], in0=sign[:], scalar=-1.0, in1=g, op0=ALU.add, op1=ALU.mult)
            link(m)
            for gate, sign, size, g in gates:
                m = dve.tensor_scalar(size[:], size[:], MOD_MIN, None, ALU.max)
            link(m)
            for gate, sign, size, g in gates:
                m = dve.scalar_tensor_tensor(out=gate[:], in0=sign[:], scalar=-1.0, in1=size[:],
                                             op0=ALU.add, op1=ALU.mult)
            m.then_inc(mod_done, 1)
            dve.wait_ge(ident_made, 9)
            dve.tensor_copy(ident_r[:], ident[:]).then_inc(ident_cast, 1)
            for padded in upto_t + upto_e:
                dve.memset(padded[:], 0.0)
            dve.wait_ge(turn_full, NC)
            dve.memset(accT[:], 0.0).then_inc(acc_zeroed, 1)
            dve.wait_ge(acc_zeroed, 1)

            def run(pair, steps):
                def full(s):
                    dve.wait_ge(bank_full[s.bank], pair * uses[s.bank] + s.use + 1)

                bcast = {s.g: s for s in steps if s.kind == "bcast"}
                for s in steps:
                    if s.kind == "proj":
                        dve.wait_ge(hi_ready, pair * counts["proj"] + s.own * counts["proj"] + s.n + 1)
                        cols = slice(s.c * BANK, (s.c + 1) * BANK)
                        for h in range(2):
                            whole = ps_ring[own_half(h), s.bank, :]
                            if s.j == 0:
                                m = dve.scalar_tensor_tensor(
                                    out=q_split[h][own_half(1 - h), cols], in0=whole, scalar=Q_SCALE,
                                    in1=q_split[h][own_half(h), cols].bitcast(F32), op0=ALU.mult, op1=ALU.subtract)
                            else:
                                m = dve.tensor_tensor(k_split[h][own_half(h), 1, cols], whole,
                                                      k_split[h][own_half(h), 0, cols].bitcast(F32), ALU.subtract)
                        m.then_inc(bank_free[s.bank], 1)
                    elif s.kind == "score":
                        full(s)
                        k0, w = piece(s.g, s.r, s.c)
                        n = chunks(s.g)
                        if s.r == 0 and s.c == 0 and (s.g or s.own):
                            turned = sum(2 * g + 2 for g in range(s.g - 1)) if s.g else -2 * GROUPS
                            dve.wait_ge(pT_full, pair * counts["turn"] + s.own * counts["turn"] + turned + PRIMED)
                        if s.c == n - 1:
                            dve.sem_inc(masks_begun, 1)
                        row = probs[:, s.g % 2, s.r, k0:k0 + w]
                        highest = row_max[:, s.g, s.r, s.c:s.c + 1]
                        if s.c < n - 1:
                            m = dve.tensor_scalar(row, ps_ring[:, s.bank, 0:w], 1.0, LOWEST, ALU.mult, ALU.max,
                                                  accum_out=highest)
                        else:
                            m = dve.tensor_tensor_reduce(row, ps_ring[:, s.bank, 0:w], causal[:, BANK - w:],
                                                         1.0, LOWEST, ALU.add, ALU.max, highest)
                        m.then_inc(bank_free[s.bank], 1)
                        if s.c == n - 1:
                            dve.wait_ge(bank_free[s.bank], pair * uses[s.bank] + s.use + 1 + PRIMED)
                            dve.tensor_reduce(neg_max[:, s.g, s.r:s.r + 1], row_max[:, s.g, s.r, 0:n], AX.X,
                                              ALU.max, negate=True).then_inc(negmax_ready, 1)
                    elif s.kind == "sum":
                        dve.wait_ge(exp_done, pair * (4 * GROUPS) + 4 * (s.own * GROUPS + s.g) + 4)
                        at = pair * (2 * GROUPS) + 2 * (s.own * GROUPS + s.g)
                        dve.reciprocal(rinv[:, s.g, :], row_sum[:, s.g, :]).then_inc(sums_step, 1)
                        dve.wait_ge(sums_step, at + 1)
                        wide = rinv[:, s.g, :].unsqueeze(2).broadcast_to([P, 4, D])
                        dve.tensor_copy(rinv_hi[:, s.g % 2], wide).then_inc(sums_step, 1)
                        dve.wait_ge(sums_step, at + 2)
                        dve.tensor_tensor(rinv_lo[:, s.g % 2], wide, rinv_hi[:, s.g % 2].bitcast(F32),
                                          ALU.subtract).then_inc(rinv_ready, 1)
                    elif s.kind == "turn" and not TURN_BY_ACT[s.n % TURN_BANKS]:
                        bank = s.n % TURN_BANKS
                        dve.wait_ge(pT_full, pair * counts["turn"] + s.n + 1 + PRIMED)
                        dve.wait_ge(pv_done, pair * counts["pv"] + max(0, s.n - TURN_BANKS + 1) + PRIMED)
                        lo = 0 if s.j <= 2 * s.g else QG
                        dve.tensor_copy(pT[:, bank, lo:BANK], ps_turn[:, bank, lo:BANK]).then_inc(pT_taken[bank], 1)
                    elif s.kind == "norm":
                        dve.wait_ge(pv_done, pair * counts["pv"] + sum(2 * g + 2 for g in range(s.g + 1)) + PRIMED)
                        b = bcast[s.g]
                        dve.wait_ge(bank_free[b.bank], pair * uses[b.bank] + b.use + 1 + PRIMED)
                        dve.tensor_tensor(oT[:, s.g * QG:(s.g + 1) * QG], ps_o[:, 0:QG], rinv_b[:, s.g % 2, :],
                                          ALU.mult).then_inc(o_ready, 1)
                    elif s.kind == "out":
                        full(s)
                        cols = slice(s.c * BANK, (s.c + 1) * BANK)
                        dve.tensor_tensor(accT[:, cols], ps_ring[:, s.bank, :], accT[:, cols],
                                          ALU.add).then_inc(bank_free[s.bank], 1)
                    elif s.kind == "back":
                        full(s)
                        xs = x_sb[:, TPC * s.c:TPC * s.c + TPC, :].rearrange("p t d -> p (t d)")
                        dve.tensor_tensor(xs, ps_ring[:, s.bank, :], xs, ALU.add).then_inc(bank_free[s.bank], 1)
                        dve.wait_ge(bank_free[s.bank], pair * uses[s.bank] + s.use + 1 + PRIMED)
                        take_stats(range(TPC * s.c, TPC * s.c + TPC))

            run(0, before)
            with dve.Fori(0, PAIRS - 1) as pair:
                run(pair, steps)
            run(PAIRS - 1, last)

            dve.wait_ge(small_turned, 1)
            dve.tensor_copy(experts[:, :, 2 * FF:2 * FF + FT],
                            ps_five[:, 4, 0:NE * FT].rearrange("p (e f) -> p e f", e=NE))
            dve.tensor_copy(wrT[:], ps_five[:, 4, NE * FT:NE * FT + NE]).then_inc(small_ready, 1)
            normalise(1, rows)
            dve.tensor_copy(rows[:, :, E:ROW].bitcast(I32), token_nos[:].unsqueeze(2)).then_inc(numbered, 1)
            dve.wait_ge(logits_full, 1)
            dve.wait_ge(late_in, 16 * 4)
            link(dve.tensor_tensor(logits[:], ps_o[:, 0:T * NE].rearrange("p (t n) -> p t n", t=T),
                                   br_b[:].unsqueeze(1).broadcast_to([P, T, NE]), ALU.add))
            link(dve.tensor_reduce(top[:], logits[:], AX.X, ALU.max))
            link(dve.tensor_tensor(is_top[:], logits[:], top[:].unsqueeze(2).broadcast_to([P, T, NE]), ALU.is_equal))
            link(dve.tensor_tensor(top_no[:], is_top[:], expert_no[:].unsqueeze(1).broadcast_to([P, T, NE]), ALU.mult))
            link(dve.tensor_reduce(first_no[:], top_no[:], AX.X, ALU.min))
            dve.tensor_tensor(onehot[:], expert_no[:].unsqueeze(1).broadcast_to([P, T, NE]),
                              first_no[:].unsqueeze(2).broadcast_to([P, T, NE]), ALU.is_equal).then_inc(onehot_ready, 1)


            by_t = lambda ap: ap.unsqueeze(1).broadcast_to([P, T, NE])
            dve.wait_ge(onehot_ready, 1)
            dve.wait_ge(sort_full, 1)
            link(dve.tensor_copy(upto_t[0][:, PAD_T:, :], ps_two[:, 1, 0:T * NE].rearrange("p (t n) -> p t n", t=T)))
            at, shift = 0, 1
            while shift < T:
                link(dve.tensor_tensor(upto_t[1 - at][:, PAD_T:, :], upto_t[at][:, PAD_T:, :],
                                       upto_t[at][:, PAD_T - shift:PAD_T + T - shift, :], ALU.add))
                at, shift = 1 - at, 2 * shift
            counted = upto_t[at]
            link(dve.tensor_tensor(above[:], counted[:, PAD_T + T - 1, :].unsqueeze(2).broadcast_to([P, NE, T]),
                                   steps_of_p[:].unsqueeze(1).broadcast_to([P, NE, T]), ALU.is_gt))
            link(dve.tensor_reduce(upto_e[0][:, PAD_E:], above[:], AX.X, ALU.add))
            at, shift = 0, 1
            while shift < NE:
                link(dve.tensor_tensor(upto_e[1 - at][:, PAD_E:], upto_e[at][:, PAD_E:],
                                       upto_e[at][:, PAD_E - shift:PAD_E + NE - shift], ALU.add))
                at, shift = 1 - at, 2 * shift
            ends = upto_e[at]
            link(dve.tensor_tensor(slot_parts[:], ps_two[:, 0, 0:T * NE].rearrange("p (t n) -> p t n", t=T),
                                   counted[:, PAD_T - 1:PAD_T + T - 1, :], ALU.add))
            link(dve.scalar_tensor_tensor(out=slot_parts[:], in0=by_t(ends[:, PAD_E - 1:PAD_E + NE - 1]),
                                          scalar=float(P), in1=slot_parts[:], op0=ALU.mult, op1=ALU.add))
            link(dve.tensor_tensor(slot_parts[:], slot_parts[:], onehot[:], ALU.mult))
            link(dve.tensor_reduce(slot_f[:], slot_parts[:], AX.X, ALU.add))
            dve.tensor_copy(slot[:], slot_f[:]).then_inc(slots_ready, 1)
            link(dve.tensor_tensor(ended[:], ends[:, PAD_E:].unsqueeze(1).broadcast_to([P, SLOTS + CHOSEN, NE]),
                                   tile_nos[:].unsqueeze(2).broadcast_to([P, SLOTS + CHOSEN, NE]), ALU.is_le))
            link(dve.tensor_reduce(expert_f[:], ended[:], AX.X, ALU.add))
            link(dve.tensor_scalar(expert_f[:], expert_f[:], float(NE - 1), None, ALU.min))
            dve.tensor_copy(tile_expert[:], expert_f[:]).then_inc(chosen_known, 1)

            dve.wait_ge(w_copied, 2 * NE)
            dve.wait_ge(w_turned, 2 * NE)
            dve.wait_ge(w2_in, 32)
            dve.wait_ge(chosen_known, 1)

            def copy_expert(i, slot_no):
                expert = dve.value_load(tile_expert[0:1, bass.ds(i, 1)], min_val=0, max_val=NE - 1)
                dve.tensor_copy(chosen[:, slot_no:slot_no + 1, :],
                                experts[:, bass.ds(expert, 1), :]).then_inc(expert_copied, 1)

            for at, n in ((FF, FT), (2 * FF + FT, 1)):
                for e in range(NE):
                    w = experts[:, e, at:at + n * E].rearrange("p (n d) -> p n d", n=n)
                    m = dve.tensor_tensor(w, w, gate_b[:].unsqueeze(1).broadcast_to([P, n, E]), ALU.mult)
            link(m)
            for i in range(CHOSEN):
                copy_expert(i, i)
            with dve.Fori(0, ROUNDS) as rnd:
                for k in range(BODY):
                    dve.wait_ge(y_full, rnd * BODY + k + 1 + PRIMED)
                    dve.wait_ge(y_stored[k % 4], rnd * (16 * BODY // 4) + stored(k - 4))
                    dve.tensor_tensor(tile_y[:, k % 4, :], ps_five[:, 2 + k % 2, 0:E],
                                      chosen[:, k % CHOSEN, 2 * FF + FT:EXPERT], ALU.add).then_inc(y_taken, 1)
                    dve.wait_ge(y_taken, rnd * BODY + k + 1 + PRIMED)
                    copy_expert(rnd * BODY + k + CHOSEN, k % CHOSEN)

            for c in range(NC):
                dve.wait_ge(y_in[c], 16)
                part = y_back[:, TPC * c:TPC * c + TPC, :]
                dve.tensor_tensor(part, part, x_sb[:, TPC * c:TPC * c + TPC, :], ALU.add).then_inc(out_ready, 1)


_INS = ['L0_attn_x', 'L0_attn_w_qkv', 'L0_attn_w_out', 'L0_ffn_Wr', 'L0_ffn_br', 'L0_ffn_W1', 'L0_ffn_b1',
        'L0_ffn_W2', 'L0_ffn_b2', 'L0_c', 'L0_wmod']
_OUTS = [((1, 2048, 128), 'float32')]


def kernel(**inputs):
    import numpy as _np
    import concourse.bacc as _bacc
    from concourse import mybir as _mybir
    from concourse.bass_utils import run_bass_kernel_spmd as _run

    nc = _bacc.Bacc("TRN2", target_bir_lowering=False, num_devices=1)
    arrays, args = {}, []
    for name in _INS:
        a = _np.ascontiguousarray(inputs[name])
        arrays[f"in_{name}_dram"] = a
        args.append(nc.dram_tensor(f"in_{name}_dram", a.shape, _mybir.dt.from_np(a.dtype), kind="ExternalInput").ap())
    for i, (shape, dtype) in enumerate(_OUTS):
        dt = _mybir.dt.from_np(_np.dtype(dtype))
        args.append(nc.dram_tensor(f"out_{i}_dram", shape, dt, kind="ExternalOutput").ap())
    adaln_block(nc, *args)
    r = _run(nc, [arrays], core_ids=[0])
    got = tuple(r.results[0][f"out_{i}_dram"] for i in range(len(_OUTS)))
    return got[0]
```
